# Optimizing a Trainium2 kernel written in Bass

```python
import numpy as np
import jax
import jax.numpy as jnp

def _softmax(x, axis=-1):
    return jax.nn.softmax(x, axis=axis)

def _gelu(x):
    return jax.nn.gelu(x, approximate=True)

def _silu(x):
    return jax.nn.silu(x)

def _sigmoid(x):
    return jax.nn.sigmoid(x)

def _layernorm(x, axis=-1, eps=1e-05):
    m = jnp.mean(x, axis=axis, keepdims=True)
    v = jnp.var(x, axis=axis, keepdims=True)
    return (x - m) / jnp.sqrt(v + eps)

def _scatter_add(tgt, idx, src, axis=0):
    return tgt.at[idx].add(src)

def _segment_sum(src, seg, n):
    return jax.ops.segment_sum(src, seg, n)
kernel_name = 'mk_cond_seq_d1_seqx_r2_547006'

def setup_inputs(seed: int=0):
    np.random.seed(seed)
    _w = jnp.asarray

    def _rec_inputs():
        import jax
        import jax.numpy as jnp
        _rk = jax.random.key(seed)
        x = -0.0002928 + 1 * jax.random.normal(jax.random.fold_in(_rk, 1), (128, 128, 512), jnp.float32)
        _lenS = 128 - jax.random.randint(jax.random.fold_in(_rk, 7), (128,), 0, max(1, 128 // 4) + 1, jnp.int32)
        _lenS2 = 128 - jax.random.randint(jax.random.fold_in(_rk, 8), (128,), 0, max(1, 128 // 4) + 1, jnp.int32)
        cond_2048 = 0.0061147 + 1.02565 * jax.random.normal(jax.random.fold_in(_rk, 11), (128, 1024), jnp.float32)
        return (x, cond_2048)
    x, cond_2048 = _rec_inputs()

    def _L0_cond_setup():
        import jax, jax.numpy as jnp
        import numpy as np
        D = 512
        DI = 1024
        N = 16
        DT_RANK = 64
        D_CONV = 4
        EPS = 1e-05

        def _layernorm(x, g, b):
            mu = jnp.mean(x, axis=-1, keepdims=True)
            var = jnp.mean((x - mu) ** 2, axis=-1, keepdims=True)
            return (x - mu) * jax.lax.rsqrt(var + EPS) * g + b

        def _mamba(xn, in_proj_w, conv_w, conv_b, x_proj_w, dt_proj_w, dt_proj_b, A_log, D_param, out_proj_w):
            b, sl, _ = xn.shape
            xz = jnp.einsum('bsd,ed->bse', xn, in_proj_w)
            x_in, z = jnp.split(xz, 2, axis=-1)
            xt = jnp.transpose(x_in, (0, 2, 1))
            u = jax.lax.conv_general_dilated(xt, conv_w[:, None, :], (1,), [(D_CONV - 1, 0)], feature_group_count=DI, dimension_numbers=('NCH', 'OIH', 'NCH')) + conv_b[None, :, None]
            u = jax.nn.silu(jnp.transpose(u, (0, 2, 1)))
            x_dbl = jnp.einsum('bsd,ed->bse', u, x_proj_w)
            dt_r, B, C = jnp.split(x_dbl, [DT_RANK, DT_RANK + N], axis=-1)
            dt = jax.nn.softplus(jnp.einsum('bsr,dr->bsd', dt_r, dt_proj_w) + dt_proj_b)
            A = -jnp.exp(A_log)

            def step(h, inp):
                dt_t, B_t, C_t, u_t = inp
                dA = jnp.exp(dt_t[:, :, None] * A)
                h = h * dA + (dt_t * u_t)[:, :, None] * B_t[:, None, :]
                y = jnp.einsum('bdn,bn->bd', h, C_t)
                return (h, y)
            seq = (jnp.transpose(dt, (1, 0, 2)), jnp.transpose(B, (1, 0, 2)), jnp.transpose(C, (1, 0, 2)), jnp.transpose(u, (1, 0, 2)))
            h0 = jnp.zeros((b, DI, N), xn.dtype)
            _, ys = jax.lax.scan(step, h0, seq)
            y = jnp.transpose(ys, (1, 0, 2)) + u * D_param
            y = y * jax.nn.silu(z)
            return jnp.einsum('bsd,ed->bse', y, out_proj_w)
        key = jax.random.key(seed)
        ks = jax.random.split(key, 16)
        s = lambda fan: 1.0 / np.sqrt(fan)
        inp = {'x': jax.random.normal(ks[0], (2, 1024, D), jnp.float32), 'c': jax.random.normal(ks[1], (2, 2 * D), jnp.float32), 'ln_g': jnp.ones((D,), jnp.float32), 'ln_b': jnp.zeros((D,), jnp.float32), 'ada_w': jax.random.normal(ks[2], (3 * D, 2 * D), jnp.float32) * s(2 * D), 'ada_b': jnp.zeros((3 * D,), jnp.float32), 'in_proj_w': jax.random.normal(ks[3], (2 * DI, D), jnp.float32) * s(D), 'conv_w': jax.random.normal(ks[4], (DI, D_CONV), jnp.float32) * s(D_CONV), 'conv_b': jnp.zeros((DI,), jnp.float32), 'x_proj_w': jax.random.normal(ks[5], (DT_RANK + 2 * N, DI), jnp.float32) * s(DI), 'dt_proj_w': jax.random.normal(ks[6], (DI, DT_RANK), jnp.float32) * s(DT_RANK), 'dt_proj_b': jax.random.uniform(ks[7], (DI,), jnp.float32, -4.0, -2.0), 'A_log': jnp.tile(jnp.log(jnp.arange(1, N + 1, dtype=jnp.float32)), (DI, 1)), 'D_param': jnp.ones((DI,), jnp.float32), 'out_proj_w': jax.random.normal(ks[8], (D, DI), jnp.float32) * s(DI)}
        return inp
    _L0_cond_all = _L0_cond_setup()
    _L0_cond_in = {k: v for k, v in _L0_cond_all.items() if k in ('ln_g', 'ln_b', 'ada_w', 'ada_b', 'in_proj_w', 'conv_w', 'conv_b', 'x_proj_w', 'dt_proj_w', 'dt_proj_b', 'A_log', 'D_param', 'out_proj_w')}
    del _L0_cond_all
    return {'x': x, 'cond_2048': cond_2048, 'L0_cond_ln_g': _L0_cond_in['ln_g'], 'L0_cond_ln_b': _L0_cond_in['ln_b'], 'L0_cond_ada_w': _L0_cond_in['ada_w'], 'L0_cond_ada_b': _L0_cond_in['ada_b'], 'L0_cond_in_proj_w': _L0_cond_in['in_proj_w'], 'L0_cond_conv_w': _L0_cond_in['conv_w'], 'L0_cond_conv_b': _L0_cond_in['conv_b'], 'L0_cond_x_proj_w': _L0_cond_in['x_proj_w'], 'L0_cond_dt_proj_w': _L0_cond_in['dt_proj_w'], 'L0_cond_dt_proj_b': _L0_cond_in['dt_proj_b'], 'L0_cond_A_log': _L0_cond_in['A_log'], 'L0_cond_D_param': _L0_cond_in['D_param'], 'L0_cond_out_proj_w': _L0_cond_in['out_proj_w']}

def reference(x, cond_2048, L0_cond_ln_g, L0_cond_ln_b, L0_cond_ada_w, L0_cond_ada_b, L0_cond_in_proj_w, L0_cond_conv_w, L0_cond_conv_b, L0_cond_x_proj_w, L0_cond_dt_proj_w, L0_cond_dt_proj_b, L0_cond_A_log, L0_cond_D_param, L0_cond_out_proj_w):
    import jax
    import jax.numpy as jnp

    def _L0_cond_ref(x, c, ln_g, ln_b, ada_w, ada_b, in_proj_w, conv_w, conv_b, x_proj_w, dt_proj_w, dt_proj_b, A_log, D_param, out_proj_w):
        import jax, jax.numpy as jnp
        import numpy as np
        D = 512
        DI = 1024
        N = 16
        DT_RANK = 64
        D_CONV = 4
        EPS = 1e-05

        def _layernorm(x, g, b):
            mu = jnp.mean(x, axis=-1, keepdims=True)
            var = jnp.mean((x - mu) ** 2, axis=-1, keepdims=True)
            return (x - mu) * jax.lax.rsqrt(var + EPS) * g + b

        def _mamba(xn, in_proj_w, conv_w, conv_b, x_proj_w, dt_proj_w, dt_proj_b, A_log, D_param, out_proj_w):
            b, sl, _ = xn.shape
            xz = jnp.einsum('bsd,ed->bse', xn, in_proj_w)
            x_in, z = jnp.split(xz, 2, axis=-1)
            xt = jnp.transpose(x_in, (0, 2, 1))
            u = jax.lax.conv_general_dilated(xt, conv_w[:, None, :], (1,), [(D_CONV - 1, 0)], feature_group_count=DI, dimension_numbers=('NCH', 'OIH', 'NCH')) + conv_b[None, :, None]
            u = jax.nn.silu(jnp.transpose(u, (0, 2, 1)))
            x_dbl = jnp.einsum('bsd,ed->bse', u, x_proj_w)
            dt_r, B, C = jnp.split(x_dbl, [DT_RANK, DT_RANK + N], axis=-1)
            dt = jax.nn.softplus(jnp.einsum('bsr,dr->bsd', dt_r, dt_proj_w) + dt_proj_b)
            A = -jnp.exp(A_log)

            def step(h, inp):
                dt_t, B_t, C_t, u_t = inp
                dA = jnp.exp(dt_t[:, :, None] * A)
                h = h * dA + (dt_t * u_t)[:, :, None] * B_t[:, None, :]
                y = jnp.einsum('bdn,bn->bd', h, C_t)
                return (h, y)
            seq = (jnp.transpose(dt, (1, 0, 2)), jnp.transpose(B, (1, 0, 2)), jnp.transpose(C, (1, 0, 2)), jnp.transpose(u, (1, 0, 2)))
            h0 = jnp.zeros((b, DI, N), xn.dtype)
            _, ys = jax.lax.scan(step, h0, seq)
            y = jnp.transpose(ys, (1, 0, 2)) + u * D_param
            y = y * jax.nn.silu(z)
            return jnp.einsum('bsd,ed->bse', y, out_proj_w)
        ada = jnp.einsum('bc,ec->be', jax.nn.silu(c), ada_w) + ada_b
        shift, scale, gate = jnp.split(ada, 3, axis=1)
        xn = _layernorm(x, ln_g, ln_b)
        xn = xn * (1.0 + scale[:, None, :]) + shift[:, None, :]
        x_ssm = _mamba(xn, in_proj_w, conv_w, conv_b, x_proj_w, dt_proj_w, dt_proj_b, A_log, D_param, out_proj_w)
        return x + gate[:, None, :] * x_ssm
    x = _L0_cond_ref(x, cond_2048, L0_cond_ln_g, L0_cond_ln_b, L0_cond_ada_w, L0_cond_ada_b, L0_cond_in_proj_w, L0_cond_conv_w, L0_cond_conv_b, L0_cond_x_proj_w, L0_cond_dt_proj_w, L0_cond_dt_proj_b, L0_cond_A_log, L0_cond_D_param, L0_cond_out_proj_w)
    return x

_drawn_inputs = setup_inputs


def setup_inputs(seed=0):
    import zlib

    import numpy as np

    out = dict(_drawn_inputs(seed))
    spreads = {'L0_cond_ln_g': (1.0, 0.2),
     'L0_cond_ln_b': (0.0, 0.1),
     'L0_cond_ada_b': (0.0, 0.1),
     'L0_cond_conv_b': (0.0, 0.1),
     'L0_cond_D_param': (1.0, 0.2)}
    factors = {}
    for name, (base, spread) in spreads.items():
        noise = np.random.default_rng([zlib.crc32(name.encode()), seed]).standard_normal(out[name].shape)
        drawn = base * np.exp(spread * noise) if base else spread * noise
        out[name] = jnp.asarray(drawn.astype(out[name].dtype))
    for name, factor in factors.items():
        out[name] = (out[name] * factor).astype(out[name].dtype)
    return out
```

```python
from contextlib import ExitStack

import concourse.bass as bass
from concourse import mybir

P = 128
F32 = mybir.dt.float32
ALU = mybir.AluOpType
ACT = mybir.ActivationFunctionType
EPS = 1e-5

SEQS = 4
NSLOT = 8
NBC = 4
EXP_TABLES = "natural_log_exp_and_others"


def mamba_program(nc, x, cond_t, ln_g, ln_b, ada_wt, ada_b, gate_b, in_proj_wt, conv_w, conv_b, x_proj_wt,
                  dt_proj_wt, dt_proj_b, a_log, d_param, out_proj_wt, out):
    NSEQ, T, D = x.shape
    DI = conv_w.shape[0]
    N = a_log.shape[1]
    R = dt_proj_wt.shape[0]
    DC = conv_w.shape[1]
    COND = cond_t.shape[0]
    E3 = ada_wt.shape[1]
    TOK = SEQS * T
    GROUPS = NSEQ // SEQS
    KD, K, KC = D // P, DI // P, COND // P
    KH = K // 2
    STEPS = 2 * N
    PAIRS = 2 * STEPS
    UNITS = 2 * PAIRS
    XR = R + 2 * N
    AT_DT, AT_Z, AT_TURN, AT_OUT, AT_CONV, AT_XDBL, AT_NEXT_DT = 0, 4, 20, 24, 36, 55, 59
    assert T == P and TOK == 512 and D == 512 and K == 8 and N == 16 and XR < P and GROUPS % 2 == 0

    FILLS = [("dt", k) for k in range(KH, K)] + [("z", e) for e in range(K)]
    FILLS += [("turn", k) for k in range(KD)] + [("out", b) for b in range(SEQS)]
    FILLS += [("conv", e) for e in range(K)]
    FILLS += [("xdbl", 0)] + [("dt", k) for k in range(KH)]
    FIRST = [f for f in FILLS if f[0] != "out"]
    SETUP = [("ada", j) for j in range(2 * KD + 1)]
    SETUP += [("turn", k) for k in range(KD)] + [("conv", e) for e in range(K)]
    SETUP += [("xdbl", 0)] + [("dt", k) for k in range(KH)]
    LAST = [f for f in FILLS if f[0] in ("z", "out") or f[0] == "dt" and f[1] >= KH]
    TAIL = [("out", b) for b in range(SEQS)]
    assert len(SETUP) % 2 == 0

    def upto(per_group, g, extra=0):
        i, p = g
        return i * (2 * per_group) + (per_group * p + extra)

    def fill_no(g, what):
        i, p = g
        nf = len(FILLS)
        if isinstance(i, int) and i == -1:
            n = SETUP.index(what)
        elif (isinstance(i, int) and 2 * i + p == 0):
            n = len(SETUP) + FIRST.index(what)
        elif isinstance(i, int) and 2 * i + p >= GROUPS - 1:
            n = len(SETUP) + len(FIRST) + nf * (GROUPS - 2)
            n += LAST.index(what) if 2 * i + p < GROUPS else len(LAST) + TAIL.index(what)
        else:
            at = len(SETUP) + len(FIRST) + nf * (p - 1) + FILLS.index(what)
            return at % 2, i * nf + at // 2, i * (2 * nf) + at
        return n % 2, n // 2, n

    def wait(eng, sem, value):
        if isinstance(value, int) and value <= 0:
            return
        eng.wait_ge(sem, value)

    with ExitStack() as ctx:
        def sb(name, shape):
            return ctx.enter_context(nc.sbuf_tensor(name, shape, F32))

        def ps(name, shape):
            return ctx.enter_context(nc.psum_tensor(name, shape, F32))

        def sem(name):
            return ctx.enter_context(nc.semaphore(name))

        w_in = sb("w_in", [P, KD, 2 * DI])
        w_out = sb("w_out", [P, K, D])
        w_x = sb("w_x", [P, K, XR])
        w_dt = sb("w_dt", [P, DI])
        ident = sb("ident", [P, P])
        a_neg = sb("a_neg", [P, K, N])
        d_skip = sb("d_skip", [P, K])
        conv_k = sb("conv_k", [P, K, DC])
        conv_c = sb("conv_c", [P, K])
        ln_gain = sb("ln_gain", [P, KD])
        ln_bias = sb("ln_bias", [P, KD])
        ada_bias = sb("ada_bias", [P, E3 // P])
        xn_scale = sb("xn_scale", [P, KD, NSEQ])
        xn_shift = sb("xn_shift", [P, KD, NSEQ])
        act_mem = sb("act_mem", [P, 3, K, TOK])
        u = [act_mem[:, 0], act_mem[:, 1]]
        z = act_mem[:, 2]
        xs = sb("xs", [P, SEQS, D])
        xnt = sb("xnt", [P, KD, TOK])
        xdbl = sb("xdbl", [P, TOK])
        dt = sb("dt", [P, K, TOK])
        v = sb("v", [P, K, TOK])
        hbuf = sb("hbuf", [P, NSLOT, TOK])
        bc = sb("bc", [P, NBC, 2, TOK])
        gate_bc = sb("gate_bc", [P, SEQS, D])
        x_res = sb("x_res", [P, SEQS, D])
        stats = sb("stats", [P, SEQS, 6])
        moments = sb("moments", [P, SEQS, 2])
        var_eps = sb("var_eps", [P, SEQS])
        rstd = sb("rstd", [P, SEQS])
        newton = sb("newton", [P, SEQS])
        w_ada = act_mem[:, :, :, :].rearrange("p a k t -> p (a k t)").rearrange("p (c e) -> p c e", c=KC)
        cond_s = dt[:, 0:2, :].rearrange("p k t -> p (k t)").rearrange("p (c b) -> p c b", c=KC)
        one_scale = v[:, 0, :].rearrange("p (k b) -> p k b", k=KD)
        gate_rows = v[:, 1, :]
        gate_bias = v[:, 2, :]

        y_acc = ps("y_acc", [P, KH, TOK])
        decay = ps("decay", [P, 2, TOK])
        bank = ps("bank", [P, 2, TOK])

        gate_dram = nc.dram_tensor("gate_rows_dram", (NSEQ, D), F32, kind="Internal").ap()
        bc_dram = nc.dram_tensor("bc_dram", (2, 2 * N, TOK), F32, kind="Internal").ap()

        s_weights = sem("weights_loaded")
        s_wada = sem("ada_weights_loaded")
        s_win = sem("w_in_loaded")
        s_ident = sem("identity_made")
        s_set = sem("constants_set")
        s_cond = sem("cond_silu_made")
        s_ada = sem("ada_steps")
        s_gate_st = sem("gate_rows_stored")
        s_x = sem("x_loaded")
        s_ln = sem("norm_steps")
        s_rstd = sem("rstd_steps")
        s_filled = sem("bank_filled")
        s_free = [sem("bank0_free"), sem("bank1_free")]
        s_tap = sem("first_tap_made")
        s_conv = sem("conv_taps")
        s_u = sem("u_made")
        s_bcst = sem("bc_stored")
        s_bc = [sem(f"bc{j}_loaded") for j in range(NBC)]
        s_sp = sem("softplus_steps")
        s_dt = sem("dt_and_v_made")
        s_decay = sem("decays_made")
        s_drive = sem("drives_made")
        s_scan = sem("scans_done")
        s_hc = sem("hc_made")
        s_sum = sem("units_summed")
        s_y = sem("y_made")
        s_z = sem("silu_z_made")
        s_gated = sem("y_gated")
        s_res = sem("residual_loaded")
        s_oadd = sem("outputs_added")
        s_out = sem("out_stored")

        x_tok = x.rearrange("(g b) t d -> g t b d", b=SEQS)
        out_tok = out.rearrange("(g b) t d -> g t b d", b=SEQS)
        gate_g = gate_dram.rearrange("(g b) d -> g b d", b=SEQS)

        N_ADA_DMAS, N_WEIGHT_DMAS = 6, 8
        ADA_STEPS = 4 * KD + 2
        NORM_STEPS = 3 * SEQS + 5

        def seq3(ap):
            return ap.rearrange("p (b t) -> p b t", b=SEQS)

        block = ctx.enter_context(nc.Block())

        def store_bc(sp, g):
            i, p = g
            b, used, n = fill_no(g, ("xdbl", 0))
            wait(sp, s_free[b], used + 1)
            sp.dma_start(bc_dram[1 - p], xdbl[R:XR, :]).then_inc(s_bcst, 16)

        def load_bc(sp, g, s):
            i, p = g
            n = s % N
            par = p if s < STEPS else 1 - p
            if s == STEPS:
                wait(sp, s_bcst, upto(16, g, 32))
            else:
                wait(sp, s_hc, upto(UNITS, g, 4 * (s - NBC) + 4))
            sp.dma_start(bc[:, s % NBC], bc_dram[par, n:2 * N:N].partition_broadcast(P)) \
                .then_inc(s_bc[s % NBC], 16)

        def load_residual(sp, g):
            i, p = g
            wait(sp, s_out, upto(16, g))
            sp.dma_start(x_res[:], x_tok[2 * i + p]).then_inc(s_res, 16)
            wait(sp, s_hc, upto(UNITS, g, 4 * (STEPS - NBC) + 4))
            sp.dma_start(gate_bc[:], gate_g[2 * i + p].partition_broadcast(P)).then_inc(s_res, 16)

        def store_out(sp, g):
            i, p = g
            wait(sp, s_oadd, upto(SEQS, g, SEQS))
            sp.dma_start(out_tok[2 * i + p], x_res[:]).then_inc(s_out, 16)

        def run_groups(eng, group):
            group((0, 0), True, False)
            group((0, 1), False, False)
            with eng.Fori(1, GROUPS // 2 - 1) as i:
                group((i, 0), False, False)
                group((i, 1), False, False)
            group((GROUPS // 2 - 1, 0), False, False)
            group((GROUPS // 2 - 1, 1), False, True)

        def before(g):
            i, p = g
            return (i, p - 1) if p else (i - 1, 1)

        def after(g):
            i, p = g
            return (i + 1, 0) if p else (i, 1)

        @block.sync
        def _(sp):
            sp.dma_start(xs[:], x_tok[0]).then_inc(s_x, 16)
            for dst, src in (
                (cond_s, cond_t.rearrange("(c p) b -> p c b", p=P)),
                (ln_gain[:], ln_g),
                (ln_bias[:], ln_b),
                (ada_bias[:], ada_b),
                (gate_bias, gate_b.partition_broadcast(P)),
                (w_ada, ada_wt.rearrange("(c p) e -> p c e", p=P)),
            ):
                sp.dma_start(dst, src).then_inc(s_wada, 16)
            sp.dma_start(w_in[:], in_proj_wt.rearrange("(k p) e -> p k e", p=P)).then_inc(s_win, 16)
            for dst, src in (
                (conv_k[:], conv_w.rearrange("(k p) j -> p k j", p=P)),
                (conv_c[:], conv_b),
                (a_neg[:], a_log.rearrange("(k p) n -> p k n", p=P)),
                (d_skip[:], d_param),
                (w_x[:], x_proj_wt.rearrange("(k p) e -> p k e", p=P)),
                (w_out[:], out_proj_wt.rearrange("(k p) e -> p k e", p=P)),
            ):
                sp.dma_start(dst, src).then_inc(s_weights, 16)
            sp.wait_ge(s_set, 4)
            sp.dma_start(w_dt[0:R, :], dt_proj_wt).then_inc(s_weights, 16)
            sp.dma_start(w_dt[XR:XR + 1, :], dt_proj_b).then_inc(s_weights, 16)
            sp.wait_ge(s_ada, ADA_STEPS)
            sp.dma_start(gate_dram, gate_rows).then_inc(s_gate_st, 16)
            sp.wait_ge(s_gate_st, 16)
            store_bc(sp, (-1, 1))
            sp.wait_ge(s_bcst, 16)
            for s in range(NBC):
                load_bc(sp, (0, 0), s)
            sp.dma_start(xs[:], x_tok[1]).then_inc(s_x, 16)

            def group(g, first, last):
                i, p = g
                for s in range(STEPS):
                    if not first and s == 21:
                        store_out(sp, before(g))
                    if not last and s == 14 and (not isinstance(i, int) or 2 * i + p + 2 < GROUPS):
                        load_x(sp, g)
                    if not last and s == STEPS - NBC:
                        store_bc(sp, g)
                    if s == STEPS - NBC:
                        load_residual(sp, g)
                    if s < STEPS - NBC or not last:
                        load_bc(sp, g, s + NBC)

            def load_x(sp, g):
                i, p = g
                wait(sp, s_filled, fill_no(g, ("turn", KD - 1))[2] + 1)
                sp.dma_start(xs[:], x_tok[2 * i + p + 2]).then_inc(s_x, 16)

            run_groups(sp, group)
            store_out(sp, (GROUPS // 2 - 1, 1))
            sp.wait_ge(s_out, 16 * GROUPS)

        @block.tensor
        def _(pe):
            def take_bank(g, what):
                b, used, _ = fill_no(g, what)
                wait(pe, s_free[b], used)
                return bank[:, b]

            def wait_read(g, what):
                b, used, _ = fill_no(g, what)
                wait(pe, s_free[b], used + 1)

            def turn(g, k):
                o = take_bank(g, ("turn", k))
                if k == 0:
                    wait(pe, s_ln, upto(NORM_STEPS, after(g), NORM_STEPS))
                for b in range(SEQS):
                    mm = pe.transpose(o[:, b * T:(b + 1) * T], xs[:, b, k * P:(k + 1) * P], ident[:])
                mm.then_inc(s_filled, 1)

            def project(g, what, e, ks):
                if 0 in ks:
                    take_bank(g, what)
                if what == ("conv", 0) and 0 in ks:
                    wait_read(g, ("turn", KD - 2))
                    wait_read(g, ("turn", KD - 1))
                b, _, _ = fill_no(g, what)
                for k in ks:
                    mm = pe.matmul(bank[:, b], w_in[:, k, e * P:(e + 1) * P], xnt[:, k],
                                   start=(k == 0), stop=(k == KD - 1))
                if KD - 1 in ks:
                    mm.then_inc(s_filled, 1)

            def x_proj(g, ks):
                if 0 in ks:
                    take_bank(g, ("xdbl", 0))
                b, _, _ = fill_no(g, ("xdbl", 0))
                wait(pe, s_u, upto(2, after(g), 2 if ks[-1] >= KH else 1))
                for k in ks:
                    mm = pe.matmul(bank[0:XR, b], w_x[:, k], u[1 - g[1]][:, k], start=(k == 0), stop=(k == K - 1))
                if K - 1 in ks:
                    mm.then_inc(s_filled, 1)

            def dt_tile(g, k):
                o = take_bank(g, ("dt", k))
                if k == 0:
                    wait_read(g, ("xdbl", 0))
                pe.matmul(o, w_dt[:, k * P:(k + 1) * P], xdbl[:], start=True, stop=True).then_inc(s_filled, 1)

            def out_tile(g, b, ks):
                if 0 in ks:
                    take_bank(g, ("out", b))
                    if b == 0:
                        wait(pe, s_gated, upto(K, before(g), K))
                bk, _, _ = fill_no(g, ("out", b))
                for k in ks:
                    mm = pe.matmul(bank[:, bk], u[1 - g[1]][:, k, b * T:(b + 1) * T], w_out[:, k],
                                   start=(k == 0), stop=(k == K - 1))
                if K - 1 in ks:
                    mm.then_inc(s_filled, 1)

            def add_states(g, c):
                half, n, kb = c // (4 * N), c // 4 % N, c % 4
                if n == 0:
                    wait(pe, s_y, upto(K, g, KH * half - KH + kb + 1))
                wait(pe, s_hc, upto(UNITS, g, c + 1))
                pe.matmul(y_acc[:, kb], ident[:], hbuf[:, c % NSLOT], start=(n == 0), stop=(n == N - 1)) \
                    .then_inc(s_sum, 1)

            g = (-1, 1)
            pe.wait_ge(s_ident, 2)
            pe.wait_ge(s_wada, 16 * N_ADA_DMAS)
            pe.wait_ge(s_cond, 1)
            for j in range(2 * KD):
                o = take_bank(g, ("ada", j))
                for c in range(KC):
                    mm = pe.matmul(o[:, 0:NSEQ], w_ada[:, c, j * P:(j + 1) * P], cond_s[:, c],
                                   start=(c == 0), stop=(c == KC - 1))
                mm.then_inc(s_filled, 1)
            o = take_bank(g, ("ada", 2 * KD))
            for c in range(KC):
                mm = pe.matmul(o, cond_s[:, c], w_ada[:, c, 2 * D:3 * D], start=(c == 0), stop=(c == KC - 1))
            mm.then_inc(s_filled, 1)
            for k in range(KD):
                turn(g, k)
            pe.wait_ge(s_win, 16)
            for e in range(K):
                project(g, ("conv", e), e, range(KD))
            pe.wait_ge(s_weights, 16 * N_WEIGHT_DMAS)
            x_proj(g, range(K))
            for k in range(KH):
                dt_tile(g, k)

            def group(g, first, last):
                for h in range(PAIRS):
                    if h < AT_Z:
                        dt_tile(g, KH + h - AT_DT)
                    elif h < AT_TURN:
                        e = (h - AT_Z) // 2
                        project(g, ("z", e), K + e, ((0, 1), (2, 3))[h % 2])
                    elif h < AT_OUT:
                        if not last:
                            turn(g, h - AT_TURN)
                    elif h < AT_CONV:
                        if not first:
                            out_tile(g, (h - AT_OUT) // 3, ((0, 1, 2), (3, 4, 5), (6, 7))[(h - AT_OUT) % 3])
                    elif last:
                        pass
                    elif h < AT_CONV + 2 * K:
                        e = (h - AT_CONV) // 2
                        project(g, ("conv", e), e, ((0, 1), (2, 3))[h % 2])
                    elif AT_XDBL <= h < AT_XDBL + 3:
                        x_proj(g, ((0, 1, 2), (3, 4, 5), (6, 7))[h - AT_XDBL])
                    elif AT_NEXT_DT <= h < AT_NEXT_DT + KH:
                        dt_tile(g, h - AT_NEXT_DT)
                    add_states(g, 2 * h)
                    add_states(g, 2 * h + 1)

            run_groups(pe, group)
            g = (GROUPS // 2, 0)
            for b in range(SEQS):
                out_tile(g, b, range(K))

        @block.scalar
        def _(act):
            def decay_tile(g, c):
                half, n = c // (4 * N), c // 4 % N
                k = half * KH + c % 4
                if n == 0:
                    wait(act, s_dt, upto(2 * K, g, 2 * k + 2))
                wait(act, s_scan, upto(UNITS, g, c - 1))
                nc.scalar.activation(seq3(decay[:, c % 2])[:, :, 1:T], seq3(dt[:, k])[:, :, 1:T], ACT.Exp,
                                     scale=a_neg[:, k, n:n + 1]).then_inc(s_decay, 1)

            def softplus(g, k, r):
                ga = g if k >= KH else after(g)
                b, used, n = fill_no(g, ("dt", k))
                if r == 0:
                    wait(act, s_filled, n + 1)
                    nc.scalar.activation(dt[:, k], bank[:, b], ACT.Abs).then_inc(s_sp, 1)
                if r == 1:
                    wait(act, s_sp, upto(3 * K, ga, 3 * k + 1))
                    nc.scalar.activation(dt[:, k], dt[:, k], ACT.Exp, scale=-1.0).then_inc(s_sp, 1)
                if r == 2:
                    wait(act, s_sp, upto(3 * K, ga, 3 * k + 2))
                    nc.scalar.activation(dt[:, k], dt[:, k], ACT.Ln, bias=1.0).then_inc(s_sp, 1)

            def first_root(g):
                ga = after(g)
                wait(act, s_ln, upto(NORM_STEPS, ga, 2 * SEQS + 1))
                nc.scalar.activation(rstd[:], var_eps[:], ACT.Ln).then_inc(s_rstd, 1)
                wait(act, s_rstd, upto(2, ga, 1))
                nc.scalar.activation(rstd[:], rstd[:], ACT.Exp, scale=-0.5).then_inc(s_rstd, 1)

            def copy_z(g, e):
                b, used, n = fill_no(g, ("z", e))
                if e == 0:
                    wait(act, s_gated, upto(K, g))
                wait(act, s_filled, n + 1)
                nc.scalar.activation(z[:, e], bank[:, b], ACT.Copy).then_inc(s_free[b], 1)

            def xn_tile(g, k):
                i, p = g
                b, used, n = fill_no(g, ("turn", k))
                wait(act, s_filled, n + 1)
                for j in range(SEQS):
                    col = i * (2 * SEQS) + ((p + 1) * SEQS + j)
                    a = nc.scalar.activation(xnt[:, k, j * T:(j + 1) * T], bank[:, b, j * T:(j + 1) * T],
                                             ACT.Identity, scale=xn_scale[:, k, bass.ds(col, 1)],
                                             bias=xn_shift[:, k, bass.ds(col, 1)])
                a.then_inc(s_free[b], 1)

            def first_tap(g, e):
                b, used, n = fill_no(g, ("conv", e))
                wait(act, s_filled, n + 1)
                nc.scalar.activation(u[1 - g[1]][:, e], bank[:, b], ACT.Identity, scale=conv_k[:, e, DC - 1:DC],
                                     bias=conv_c[:, e:e + 1]).then_inc(s_tap, 1)

            def silu_u(g, half):
                for e in (KH * half + KH - 2, KH * half + KH - 1):
                    b, used, n = fill_no(g, ("conv", e))
                    wait(act, s_free[b], used + 1)
                t = u[1 - g[1]][:, half * KH:half * KH + KH]
                nc.scalar.activation(t, t, ACT.Silu).then_inc(s_u, 1)

            def silu_z(g, half):
                if half == 0:
                    for e in (K - 2, K - 1):
                        b, used, n = fill_no(g, ("z", e))
                        wait(act, s_free[b], used + 1)
                t = z[:, half * KH:half * KH + KH]
                nc.scalar.activation(t, t, ACT.Silu).then_inc(s_z, 1)

            def copy_xdbl(g):
                b, used, n = fill_no(g, ("xdbl", 0))
                wait(act, s_bcst, upto(16, g, 16))
                wait(act, s_filled, n + 1)
                nc.scalar.activation(xdbl[0:XR, :], bank[0:XR, b], ACT.Copy).then_inc(s_free[b], 1)

            nc.scalar.preload_act_table_set(EXP_TABLES)
            g = (-1, 1)
            first_root(g)
            act.wait_ge(s_wada, 16 * N_ADA_DMAS)
            nc.scalar.activation(cond_s, cond_s, ACT.Silu).then_inc(s_cond, 1)
            act.wait_ge(s_ada, ADA_STEPS)
            for k in range(KD):
                xn_tile(g, k)
            act.wait_ge(s_weights, 16 * N_WEIGHT_DMAS)
            for e in range(K):
                first_tap(g, e)
            silu_u(g, 0)
            silu_u(g, 1)
            copy_xdbl(g)
            nc.scalar.preload_act_table_set(EXP_TABLES)
            nc.scalar.activation(a_neg[:], a_neg[:], ACT.Exp).then_inc(s_cond, 1)
            for k in range(KH):
                for r in range(3):
                    softplus(g, k, r)
            act.wait_ge(s_set, 6)

            def group(g, first, last):
                for h in range(PAIRS):
                    if h == AT_XDBL and not last:
                        silu_u(g, 0)
                        silu_u(g, 1)
                        nc.scalar.preload_act_table_set(EXP_TABLES)
                    if h == AT_Z + 2 * K + 6:
                        silu_z(g, 0)
                        silu_z(g, 1)
                        nc.scalar.preload_act_table_set(EXP_TABLES)
                    decay_tile(g, 2 * h)
                    if h == 0 and not first:
                        softplus(before(g), KH - 1, 2)
                    if 3 <= h < 3 + KH:
                        softplus(g, KH + h - 3, 2)
                    if not last and AT_NEXT_DT + 2 <= h:
                        softplus(g, h - AT_NEXT_DT - 2, 2)
                    if 2 <= h < 2 + KH:
                        softplus(g, KH + h - 2, 0)
                    if not last and AT_NEXT_DT + 1 <= h:
                        softplus(g, h - AT_NEXT_DT - 1, 0)
                    if AT_Z + 3 <= h < AT_Z + 3 + 2 * K and (h - AT_Z) % 2 == 1:
                        copy_z(g, (h - AT_Z - 3) // 2)
                    if not last:
                        if h == AT_TURN - 6:
                            first_root(g)
                        if AT_TURN + 1 <= h < AT_TURN + 1 + KD:
                            xn_tile(g, h - AT_TURN - 1)
                        if AT_CONV + 3 <= h < AT_CONV + 3 + 2 * K and (h - AT_CONV) % 2 == 1:
                            first_tap(g, (h - AT_CONV - 3) // 2)
                        if h == AT_XDBL + 3:
                            copy_xdbl(g)
                    decay_tile(g, 2 * h + 1)
                    if 2 <= h < 2 + KH:
                        softplus(g, KH + h - 2, 1)
                    if not last and AT_NEXT_DT + 1 <= h:
                        softplus(g, h - AT_NEXT_DT - 1, 1)

            run_groups(act, group)

        @block.vector
        def _(dve):
            def statistics(g, b):
                if b == 0:
                    wait(dve, s_x, upto(16, after(g), 16))
                dve.bn_stats(stats[:, b], xs[:, b]).then_inc(s_ln, 1)

            def statistics_made(g):
                wait(dve, s_ln, upto(NORM_STEPS, after(g), SEQS))

            def aggregate(g):
                for b in range(SEQS):
                    dve.bn_aggr(moments[:, b], stats[:, b]).then_inc(s_ln, 1)
                wait(dve, s_ln, upto(NORM_STEPS, after(g), 2 * SEQS))
                dve.tensor_scalar(var_eps[:], moments[:, :, 1], EPS, None, ALU.add).then_inc(s_ln, 1)

            def root(g):
                ga = after(g)
                at = 2 * SEQS + 1
                wait(dve, s_rstd, upto(2, ga, 2))
                dve.tensor_tensor(newton[:], rstd[:], rstd[:], ALU.mult).then_inc(s_ln, 1)
                wait(dve, s_ln, upto(NORM_STEPS, ga, at + 1))
                dve.tensor_tensor(newton[:], newton[:], var_eps[:], ALU.mult).then_inc(s_ln, 1)
                wait(dve, s_ln, upto(NORM_STEPS, ga, at + 2))
                dve.tensor_scalar(newton[:], newton[:], -0.5, 1.5, ALU.mult, ALU.add).then_inc(s_ln, 1)
                wait(dve, s_ln, upto(NORM_STEPS, ga, at + 3))
                dve.tensor_tensor(rstd[:], rstd[:], newton[:], ALU.mult).then_inc(s_ln, 1)

            def normalise(g, b):
                if b == 0:
                    wait(dve, s_ln, upto(NORM_STEPS, after(g), 2 * SEQS + 5))
                dve.tensor_scalar(xs[:, b], xs[:, b], moments[:, b, 0:1], rstd[:, b:b + 1],
                                  ALU.subtract, ALU.mult).then_inc(s_ln, 1)

            def tap(g, e, j):
                b, used, n = fill_no(g, ("conv", e))
                back = j + 1
                if j == 0:
                    wait(dve, s_tap, upto(K, after(g), e + 1))
                else:
                    wait(dve, s_conv, upto(2 * K, after(g), 2 * e + j))
                acc = seq3(u[1 - g[1]][:, e])[:, :, back:T]
                t = dve.scalar_tensor_tensor(acc, seq3(bank[:, b])[:, :, 0:T - back],
                                             conv_k[:, e, DC - 1 - back:DC - back], acc, ALU.mult, ALU.add)
                if back < DC - 1:
                    t.then_inc(s_conv, 1)
                else:
                    t.then_inc(s_free[b], 1)

            def finish_dt(g, k, r):
                ga = g if k >= KH else after(g)
                b, used, n = fill_no(g, ("dt", k))
                if r == 0:
                    wait(dve, s_sp, upto(3 * K, ga, 3 * k + 3))
                    dve.scalar_tensor_tensor(dt[:, k], bank[:, b], 0.0, dt[:, k], ALU.max, ALU.add) \
                        .then_inc(s_free[b], 1)
                else:
                    wait(dve, s_free[b], used + 1)
                    if k == 0:
                        wait(dve, s_u, upto(2, ga, 2))
                    dve.tensor_tensor(v[:, k], dt[:, k], u[ga[1]][:, k], ALU.mult).then_inc(s_dt, 2)

            def drive(g, h):
                if h == PAIRS:
                    g, h = after(g), 0
                s = h // 2
                half, n = s // N, s % N
                k = half * KH + 2 * (h % 2)
                if n == 0:
                    wait(dve, s_dt, upto(2 * K, g, 2 * (k + 2)))
                wait(dve, s_sum, upto(UNITS, g, 2 * h + 2 - NSLOT))
                if h % 2 == 0:
                    wait(dve, s_bc[s % NBC], upto(16 * (STEPS // NBC), g, 16 * (s // NBC + 1)))
                at = 2 * h % NSLOT
                dve.tensor_tensor(hbuf[:, at:at + 2], v[:, k:k + 2],
                                  bc[:, s % NBC, 0].unsqueeze(1).broadcast_to([P, 2, TOK]), ALU.mult) \
                    .then_inc(s_drive, 1)

            def scan(g, c):
                t = hbuf[:, c % NSLOT]
                if c % 2 == 0:
                    wait(dve, s_drive, upto(PAIRS, g, c // 2 + 1))
                wait(dve, s_decay, upto(UNITS, g, c + 1))
                dve.tensor_tensor_scan(t, decay[:, c % 2], t, 0.0, ALU.mult, ALU.add).then_inc(s_scan, 1)

            def take_y(g, half, kb):
                k = half * KH + kb
                wait(dve, s_sum, upto(UNITS, g, 4 * (half * N + N - 1) + kb + 1))
                dve.scalar_tensor_tensor(u[g[1]][:, k], u[g[1]][:, k], d_skip[:, k:k + 1], y_acc[:, kb],
                                         ALU.mult, ALU.add).then_inc(s_y, 1)

            def gate_out(g, b):
                bk, used, n = fill_no(g, ("out", b))
                if b == 0:
                    wait(dve, s_res, upto(32, before(g), 32))
                wait(dve, s_filled, n + 1)
                dve.tensor_tensor(gate_bc[:, b], bank[:, bk], gate_bc[:, b], ALU.mult).then_inc(s_free[bk], 1)

            dve.memset(w_dt[:], 0.0).then_inc(s_set, 1)
            dve.memset(xdbl[:], 0.0).then_inc(s_set, 1)
            dve.wait_ge(s_set, 2)
            dve.memset(xdbl[XR:XR + 1, :], 1.0).then_inc(s_set, 1)
            dve.memset(decay[:], 0.0).then_inc(s_set, 1)
            g = (-1, 1)
            for b in range(SEQS):
                statistics(g, b)
            statistics_made(g)
            aggregate(g)
            root(g)
            for b in range(SEQS):
                normalise(g, b)
            dve.wait_ge(s_wada, 16 * N_ADA_DMAS)
            done = 0
            dve.tensor_scalar(ada_bias[:, KD:2 * KD], ada_bias[:, KD:2 * KD], 1.0, None, ALU.add).then_inc(s_ada, 1)
            done += 1
            dve.wait_ge(s_ada, done)
            for k in range(KD):
                b, used, n = fill_no(g, ("ada", k))
                dve.wait_ge(s_filled, n + 1)
                dve.tensor_scalar(xn_shift[:, k], bank[:, b, 0:NSEQ], ada_bias[:, k:k + 1], None, ALU.add).then_inc(s_ada, 1)
                done += 1
                dve.wait_ge(s_ada, done)
                dve.sem_inc(s_free[b], 1)
            for k in range(KD):
                b, used, n = fill_no(g, ("ada", KD + k))
                dve.wait_ge(s_filled, n + 1)
                dve.tensor_scalar(one_scale[:, k], bank[:, b, 0:NSEQ], ada_bias[:, KD + k:KD + k + 1], None,
                                  ALU.add).then_inc(s_ada, 1)
                done += 1
                dve.wait_ge(s_ada, done)
                dve.sem_inc(s_free[b], 1)
                dve.tensor_scalar(xn_scale[:, k], one_scale[:, k], ln_gain[:, k:k + 1], None, ALU.mult).then_inc(s_ada, 1)
                dve.scalar_tensor_tensor(xn_shift[:, k], one_scale[:, k], ln_bias[:, k:k + 1], xn_shift[:, k],
                                         ALU.mult, ALU.add).then_inc(s_ada, 1)
                done += 2
            b, used, n = fill_no(g, ("ada", 2 * KD))
            dve.wait_ge(s_filled, n + 1)
            dve.tensor_tensor(gate_rows, bank[:, b], gate_bias, ALU.add).then_inc(s_ada, 1)
            done += 1
            dve.wait_ge(s_ada, done)
            assert done == ADA_STEPS
            dve.sem_inc(s_free[b], 1)
            dve.wait_ge(s_weights, 16 * N_WEIGHT_DMAS)
            for e in range(K):
                for j in range(3):
                    tap(g, e, j)
            dve.wait_ge(s_cond, 2)
            dve.tensor_scalar(a_neg[:], a_neg[:], -1.0, None, ALU.mult).then_inc(s_set, 2)
            dve.wait_ge(s_gate_st, 16)
            for k in range(KH):
                finish_dt(g, k, 0)
                finish_dt(g, k, 1)
            drive((0, 0), 0)

            def group(g, first, last):
                for h in range(PAIRS):
                    scan(g, 2 * h)
                    if h == 0 and not first:
                        for k in (KH - 2, KH - 1):
                            finish_dt(before(g), k, 0)
                            finish_dt(before(g), k, 1)
                    if 4 <= h < 4 + KH:
                        finish_dt(g, KH + h - 4, 0)
                    if not last and AT_NEXT_DT + 3 <= h:
                        finish_dt(g, h - AT_NEXT_DT - 3, 0)
                        finish_dt(g, h - AT_NEXT_DT - 3, 1)
                    if not last and AT_CONV + 3 <= h < AT_CONV + 4 + 2 * K:
                        e, odd = (h - AT_CONV - 3) // 2, (h - AT_CONV - 3) % 2
                        if e < K:
                            tap(g, e, 2 if odd else 0)
                    if h < PAIRS - 1 or not last:
                        drive(g, h + 1)
                    if h == AT_TURN - 7 and not last:
                        statistics_made(g)
                    scan(g, 2 * h + 1)
                    if 4 <= h < 4 + KH:
                        finish_dt(g, KH + h - 4, 1)
                    if not first and AT_OUT + 5 <= h and (h - AT_OUT - 5) % 3 == 0 and (h - AT_OUT - 5) // 3 < SEQS:
                        gate_out(g, (h - AT_OUT - 5) // 3)
                    if not last:
                        if AT_CONV + 3 <= h < AT_CONV + 4 + 2 * K:
                            e, odd = (h - AT_CONV - 3) // 2, (h - AT_CONV - 3) % 2
                            if e < K and not odd:
                                tap(g, e, 1)
                        if AT_TURN - 12 <= h < AT_TURN - 12 + SEQS:
                            statistics(g, h - (AT_TURN - 12))
                        if h == AT_TURN - 7:
                            aggregate(g)
                        if h == AT_TURN - 5:
                            root(g)
                        if AT_TURN - 4 <= h < AT_TURN:
                            normalise(g, h - (AT_TURN - 4))
                    if h == 1 and not first:
                        for kb in range(KH):
                            take_y(before(g), 1, kb)
                    if h == 2 * N + 1:
                        for kb in range(KH):
                            take_y(g, 0, kb)

            run_groups(dve, group)
            g = (GROUPS // 2, 0)
            for kb in range(KH):
                take_y(before(g), 1, kb)
            for b in range(SEQS):
                gate_out(g, b)

        @block.gpsimd
        def _(pool):
            def weigh(g, c):
                s = c // 4
                wait(pool, s_scan, upto(UNITS, g, c + 1))
                if c % 4 == 0:
                    wait(pool, s_bc[s % NBC], upto(16 * (STEPS // NBC), g, 16 * (s // NBC + 1)))
                nc.gpsimd.tensor_tensor(hbuf[:, c % NSLOT], hbuf[:, c % NSLOT], bc[:, s % NBC, 1],
                                        ALU.mult).then_inc(s_hc, 1)

            def gate_y(g, k):
                wait(pool, s_y, upto(K, g, k + 1))
                wait(pool, s_z, upto(2, g, k // KH + 1))
                nc.gpsimd.tensor_tensor(u[g[1]][:, k], u[g[1]][:, k], z[:, k], ALU.mult).then_inc(s_gated, 1)

            def add_residual(g, b):
                bk, used, n = fill_no(g, ("out", b))
                wait(pool, s_free[bk], used + 1)
                nc.gpsimd.tensor_tensor(x_res[:, b], x_res[:, b], gate_bc[:, b], ALU.add).then_inc(s_oadd, 1)

            pool.memset(ident[:], 0.0).then_inc(s_ident, 1)
            pool.wait_ge(s_ident, 1)
            pool.affine_select(out=ident[:], in_=ident[:], compare_op=ALU.not_equal, fill=1.0, base=0,
                               pattern=[[-1, P]], channel_multiplier=1).then_inc(s_ident, 1)

            def group(g, first, last):
                for h in range(PAIRS):
                    weigh(g, 2 * h)
                    if 2 <= h < 2 + KH and not first:
                        gate_y(before(g), KH + h - 2)
                    if 2 * N + 4 <= h < 2 * N + 4 + KH:
                        gate_y(g, h - 2 * N - 4)
                    weigh(g, 2 * h + 1)
                    if not first and AT_OUT + 6 <= h and (h - AT_OUT - 6) % 3 == 0 and (h - AT_OUT - 6) // 3 < SEQS:
                        add_residual(g, (h - AT_OUT - 6) // 3)

            run_groups(pool, group)
            g = (GROUPS // 2, 0)
            for k in range(KH, K):
                gate_y(before(g), k)
            for b in range(SEQS):
                add_residual(g, b)


def kernel(**inputs):
    import numpy as _np
    import concourse.bacc as _bacc
    from concourse.bass_utils import run_bass_kernel_spmd as _run

    w = {k.replace("L0_cond_", ""): _np.asarray(a) for k, a in inputs.items()}

    def by_channel(a):
        return a.reshape(-1, P).T

    laid = {
        "x": w["x"], "cond_t": w["cond_2048"].T, "ln_g": by_channel(w["ln_g"]), "ln_b": by_channel(w["ln_b"]),
        "ada_wt": w["ada_w"].T, "ada_b": by_channel(w["ada_b"]), "gate_b": w["ada_b"][-w["ln_g"].size:], "in_proj_wt": w["in_proj_w"].T,
        "conv_w": w["conv_w"], "conv_b": by_channel(w["conv_b"]), "x_proj_wt": w["x_proj_w"].T,
        "dt_proj_wt": w["dt_proj_w"].T, "dt_proj_b": w["dt_proj_b"].reshape(1, -1),
        "a_log": w["A_log"], "d_param": by_channel(w["D_param"]), "out_proj_wt": w["out_proj_w"].T,
    }
    nc = _bacc.Bacc("TRN2", target_bir_lowering=False, num_devices=1)
    arrays, args = {}, []
    for name, a in laid.items():
        a = _np.ascontiguousarray(a)
        arrays[f"in_{name}"] = a
        args.append(nc.dram_tensor(f"in_{name}", a.shape, mybir.dt.from_np(a.dtype), kind="ExternalInput").ap())
    args.append(nc.dram_tensor("out_0", w["x"].shape, F32, kind="ExternalOutput").ap())
    mamba_program(nc, *args)
    r = _run(nc, [arrays], core_ids=[0])
    return r.results[0]["out_0"]
```

```python
from contextlib import ExitStack

import concourse.bass as bass
from concourse import mybir

P = 128
F32 = mybir.dt.float32
ALU = mybir.AluOpType
ACT = mybir.ActivationFunctionType
EPS = 1e-5

SEQS = 4
NSLOT = 8
NBC = 4
EXP_TABLES = "natural_log_exp_and_others"


def mamba_program(nc, x, cond_t, ln_g, ln_b, ada_wt, ada_b, gate_b, in_proj_wt, conv_w, conv_b, x_proj_wt,
                  dt_proj_wt, dt_proj_b, a_log, d_param, out_proj_wt, out):
    NSEQ, T, D = x.shape
    DI = conv_w.shape[0]
    N = a_log.shape[1]
    R = dt_proj_wt.shape[0]
    DC = conv_w.shape[1]
    COND = cond_t.shape[0]
    E3 = ada_wt.shape[1]
    TOK = SEQS * T
    GROUPS = NSEQ // SEQS
    KD, K, KC = D // P, DI // P, COND // P
    KH = K // 2
    STEPS = 2 * N
    PAIRS = 2 * STEPS
    UNITS = 2 * PAIRS
    XR = R + 2 * N
    assert T == P and TOK == 512 and D == 512 and K == 8 and N == 16 and XR < P and GROUPS % 2 == 0

    Z_AHEAD = 4
    PRODUCTS = {"z": KD, "conv": KD, "out": K, "xdbl": K, "dt": 1, "turn": 1}
    PLAN = {h: [] for h in range(PAIRS)}
    FILLS, END = [], {}

    def lay(fills, begin, end):
        products = [(f, j) for f in fills for j in range(PRODUCTS[f[0]])]
        for n, (f, j) in enumerate(products):
            h = begin + n * (end - begin) // len(products)
            if PLAN[h] and PLAN[h][-1][0] == f:
                PLAN[h][-1] = (f, PLAN[h][-1][1], j + 1)
            else:
                PLAN[h].append((f, j, j + 1))
            END[f] = h
        FILLS.extend(fills)

    lay([("z", 4), ("dt", 4), ("z", 5), ("dt", 5), ("z", 6), ("dt", 6), ("z", 7), ("dt", 7)], 0, 10)
    lay([("out", b) for b in range(SEQS)], 10, 24)
    AT_TURN = 24
    lay([("turn", k) for k in range(KD)], 24, 27)
    lay([("conv", e) for e in range(KH)], 27, 37)
    lay([("z", 0), ("conv", 4), ("conv", 5), ("z", 1), ("conv", 6), ("conv", 7)], 37, 50)
    lay([("z", 2)], 50, 52)
    lay([("xdbl", 0)], 53, 56)
    lay([("dt", k) for k in range(KH)], 57, 57 + KH)
    lay([("z", 3)], 61, 63)
    SILU_U, SILU_Z = 53, END["z", K - 1] + 4

    def is_next(f):
        return f[0] in ("turn", "conv", "xdbl") or f == ("dt", f[1]) and f[1] < KH or f[0] == "z" and f[1] < Z_AHEAD

    FIRST = [f for f in FILLS if f[0] != "out"]
    SETUP = [("ada", j) for j in range(2 * KD + 1)]
    SETUP += [("turn", k) for k in range(KD)] + [("conv", e) for e in range(K)]
    SETUP += [("z", e) for e in range(Z_AHEAD)] + [("xdbl", 0)] + [("dt", k) for k in range(KH)]
    LAST = [f for f in FILLS if not is_next(f)]
    TAIL = [("out", b) for b in range(SEQS)]

    def due(g, h, first, last, kind, lag, late_lag=None):
        for f in FILLS:
            if f[0] == kind:
                at = END[f] + (late_lag if late_lag is not None and is_next(f) else lag)
                if at == h and not (first and kind == "out") and not (last and is_next(f)):
                    yield g, f[1]
                if at == h + PAIRS and not first:
                    yield before(g), f[1]

    def before(g):
        i, p = g
        return (i, p - 1) if p else (i - 1, 1)

    def after(g):
        i, p = g
        return (i + 1, 0) if p else (i, 1)

    def upto(per_group, g, extra=0):
        i, p = g
        return i * (2 * per_group) + (per_group * p + extra)

    def fill_no(g, what):
        i, p = g
        nf = len(FILLS)
        if isinstance(i, int) and i == -1:
            n = SETUP.index(what)
        elif (isinstance(i, int) and 2 * i + p == 0):
            n = len(SETUP) + FIRST.index(what)
        elif isinstance(i, int) and 2 * i + p >= GROUPS - 1:
            n = len(SETUP) + len(FIRST) + nf * (GROUPS - 2)
            n += LAST.index(what) if 2 * i + p < GROUPS else len(LAST) + TAIL.index(what)
        else:
            at = len(SETUP) + len(FIRST) + nf * (p - 1) + FILLS.index(what)
            return at % 2, i * nf + at // 2, i * (2 * nf) + at
        return n % 2, n // 2, n

    def wait(eng, sem, value):
        if isinstance(value, int) and value <= 0:
            return
        eng.wait_ge(sem, value)

    with ExitStack() as ctx:
        def sb(name, shape):
            return ctx.enter_context(nc.sbuf_tensor(name, shape, F32))

        def ps(name, shape):
            return ctx.enter_context(nc.psum_tensor(name, shape, F32))

        def sem(name):
            return ctx.enter_context(nc.semaphore(name))

        w_in = sb("w_in", [P, KD, 2 * DI])
        w_out = sb("w_out", [P, K, D])
        w_x = sb("w_x", [P, K, XR])
        w_dt = sb("w_dt", [P, DI])
        ident = sb("ident", [P, P])
        a_neg = sb("a_neg", [P, K, N])
        d_skip = sb("d_skip", [P, K])
        conv_k = sb("conv_k", [P, K, DC])
        conv_c = sb("conv_c", [P, K])
        ln_gain = sb("ln_gain", [P, KD])
        ln_bias = sb("ln_bias", [P, KD])
        ada_bias = sb("ada_bias", [P, E3 // P])
        xn_scale = sb("xn_scale", [P, KD, NSEQ])
        xn_shift = sb("xn_shift", [P, KD, NSEQ])
        act_mem = sb("act_mem", [P, 3, K, TOK])
        u = [act_mem[:, 0], act_mem[:, 1]]
        z = act_mem[:, 2]
        xs = sb("xs", [P, SEQS, D])
        xnt = sb("xnt", [P, KD, TOK])
        xdbl = sb("xdbl", [P, TOK])
        dt = sb("dt", [P, K, TOK])
        v = sb("v", [P, K, TOK])
        hbuf = sb("hbuf", [P, NSLOT, TOK])
        bc = sb("bc", [P, NBC, 2, TOK])
        gate_bc = sb("gate_bc", [P, SEQS, D])
        x_res = sb("x_res", [P, SEQS, D])
        stats = sb("stats", [P, SEQS, 6])
        moments = sb("moments", [P, SEQS, 2])
        var_eps = sb("var_eps", [P, SEQS])
        rstd = sb("rstd", [P, SEQS])
        newton = sb("newton", [P, SEQS])
        w_ada = act_mem[:, :, :, :].rearrange("p a k t -> p (a k t)").rearrange("p (c e) -> p c e", c=KC)
        cond_s = dt[:, 0:2, :].rearrange("p k t -> p (k t)").rearrange("p (c b) -> p c b", c=KC)
        one_scale = v[:, 0, :].rearrange("p (k b) -> p k b", k=KD)
        gate_rows = v[:, 1, :]
        gate_bias = v[:, 2, :]

        y_acc = ps("y_acc", [P, KH, TOK])
        decay = ps("decay", [P, 2, TOK])
        bank = ps("bank", [P, 2, TOK])

        gate_dram = nc.dram_tensor("gate_rows_dram", (NSEQ, D), F32, kind="Internal").ap()
        bc_dram = nc.dram_tensor("bc_dram", (2, 2 * N, TOK), F32, kind="Internal").ap()

        s_weights = sem("weights_loaded")
        s_wada = sem("ada_weights_loaded")
        s_win = sem("w_in_loaded")
        s_ident = sem("identity_made")
        s_set = sem("constants_set")
        s_cond = sem("cond_silu_made")
        s_ada = sem("ada_steps")
        s_gate_st = sem("gate_rows_stored")
        s_x = sem("x_loaded")
        s_ln = sem("norm_steps")
        s_rstd = sem("rstd_steps")
        s_filled = sem("bank_filled")
        s_free = [sem("bank0_free"), sem("bank1_free")]
        s_tap = sem("first_tap_made")
        s_conv = sem("conv_taps")
        s_u = sem("u_made")
        s_bcst = sem("bc_stored")
        s_bc = [sem(f"bc{j}_loaded") for j in range(NBC)]
        s_sp = sem("softplus_steps")
        s_dt = sem("dt_and_v_made")
        s_decay = sem("decays_made")
        s_drive = sem("drives_made")
        s_scan = sem("scans_done")
        s_hc = sem("hc_made")
        s_sum = sem("units_summed")
        s_y = sem("y_made")
        s_z = sem("silu_z_made")
        s_gated = sem("y_gated")
        s_res = sem("residual_loaded")
        s_oadd = sem("outputs_added")
        s_out = sem("out_stored")

        x_tok = x.rearrange("(g b) t d -> g t b d", b=SEQS)
        out_tok = out.rearrange("(g b) t d -> g t b d", b=SEQS)
        gate_g = gate_dram.rearrange("(g b) d -> g b d", b=SEQS)

        N_ADA_DMAS, N_WEIGHT_DMAS = 6, 8
        ADA_STEPS = 4 * KD + 2
        NORM_STEPS = 3 * SEQS + 5

        def seq3(ap):
            return ap.rearrange("p (b t) -> p b t", b=SEQS)

        block = ctx.enter_context(nc.Block())

        def store_bc(sp, g):
            i, p = g
            b, used, n = fill_no(g, ("xdbl", 0))
            wait(sp, s_free[b], used + 1)
            sp.dma_start(bc_dram[1 - p], xdbl[R:XR, :]).then_inc(s_bcst, 16)

        def load_bc(sp, g, s):
            i, p = g
            n = s % N
            par = p if s < STEPS else 1 - p
            if s == STEPS:
                wait(sp, s_bcst, upto(16, g, 32))
            else:
                wait(sp, s_hc, upto(UNITS, g, 4 * (s - NBC) + 4))
            sp.dma_start(bc[:, s % NBC], bc_dram[par, n:2 * N:N].partition_broadcast(P)) \
                .then_inc(s_bc[s % NBC], 16)

        def load_residual(sp, g):
            i, p = g
            wait(sp, s_out, upto(16, g))
            sp.dma_start(x_res[:], x_tok[2 * i + p]).then_inc(s_res, 16)
            wait(sp, s_hc, upto(UNITS, g, 4 * (STEPS - NBC) + 4))
            sp.dma_start(gate_bc[:], gate_g[2 * i + p].partition_broadcast(P)).then_inc(s_res, 16)

        def store_out(sp, g):
            i, p = g
            wait(sp, s_oadd, upto(SEQS, g, SEQS))
            sp.dma_start(out_tok[2 * i + p], x_res[:]).then_inc(s_out, 16)

        def run_groups(eng, group):
            group((0, 0), True, False)
            group((0, 1), False, False)
            with eng.Fori(1, GROUPS // 2 - 1) as i:
                group((i, 0), False, False)
                group((i, 1), False, False)
            group((GROUPS // 2 - 1, 0), False, False)
            group((GROUPS // 2 - 1, 1), False, True)

        @block.sync
        def _(sp):
            sp.dma_start(xs[:], x_tok[0]).then_inc(s_x, 16)
            for dst, src in (
                (cond_s, cond_t.rearrange("(c p) b -> p c b", p=P)),
                (ln_gain[:], ln_g),
                (ln_bias[:], ln_b),
                (ada_bias[:], ada_b),
                (gate_bias, gate_b.partition_broadcast(P)),
                (w_ada, ada_wt.rearrange("(c p) e -> p c e", p=P)),
            ):
                sp.dma_start(dst, src).then_inc(s_wada, 16)
            sp.dma_start(w_in[:], in_proj_wt.rearrange("(k p) e -> p k e", p=P)).then_inc(s_win, 16)
            for dst, src in (
                (conv_k[:], conv_w.rearrange("(k p) j -> p k j", p=P)),
                (conv_c[:], conv_b),
                (a_neg[:], a_log.rearrange("(k p) n -> p k n", p=P)),
                (d_skip[:], d_param),
                (w_x[:], x_proj_wt.rearrange("(k p) e -> p k e", p=P)),
                (w_out[:], out_proj_wt.rearrange("(k p) e -> p k e", p=P)),
            ):
                sp.dma_start(dst, src).then_inc(s_weights, 16)
            sp.wait_ge(s_set, 4)
            sp.dma_start(w_dt[0:R, :], dt_proj_wt).then_inc(s_weights, 16)
            sp.dma_start(w_dt[XR:XR + 1, :], dt_proj_b).then_inc(s_weights, 16)
            sp.wait_ge(s_ada, ADA_STEPS)
            sp.dma_start(gate_dram, gate_rows).then_inc(s_gate_st, 16)
            sp.wait_ge(s_gate_st, 16)
            store_bc(sp, (-1, 1))
            sp.wait_ge(s_bcst, 16)
            for s in range(NBC):
                load_bc(sp, (0, 0), s)
            sp.dma_start(xs[:], x_tok[1]).then_inc(s_x, 16)

            def group(g, first, last):
                i, p = g
                for s in range(STEPS):
                    if not first and s == 16:
                        store_out(sp, before(g))
                    if not last and s == 16 and (not isinstance(i, int) or 2 * i + p + 2 < GROUPS):
                        load_x(sp, g)
                    if not last and s == STEPS - NBC:
                        store_bc(sp, g)
                    if s == STEPS - NBC:
                        load_residual(sp, g)
                    if s < STEPS - NBC or not last:
                        load_bc(sp, g, s + NBC)

            def load_x(sp, g):
                i, p = g
                wait(sp, s_filled, fill_no(g, ("turn", KD - 1))[2] + 1)
                sp.dma_start(xs[:], x_tok[2 * i + p + 2]).then_inc(s_x, 16)

            run_groups(sp, group)
            store_out(sp, (GROUPS // 2 - 1, 1))
            sp.wait_ge(s_out, 16 * GROUPS)

        @block.tensor
        def _(pe):
            def take_bank(g, what):
                b, used, _ = fill_no(g, what)
                wait(pe, s_free[b], used)
                return bank[:, b]

            def wait_read(g, what):
                b, used, _ = fill_no(g, what)
                wait(pe, s_free[b], used + 1)

            def turn(g, k):
                o = take_bank(g, ("turn", k))
                if k == 0:
                    wait(pe, s_ln, upto(NORM_STEPS, after(g), NORM_STEPS))
                for b in range(SEQS):
                    mm = pe.transpose(o[:, b * T:(b + 1) * T], xs[:, b, k * P:(k + 1) * P], ident[:])
                mm.then_inc(s_filled, 1)

            def project(g, what, e, ks):
                if 0 in ks:
                    take_bank(g, what)
                if what == ("conv", 0) and 0 in ks:
                    wait_read(g, ("turn", KD - 2))
                    wait_read(g, ("turn", KD - 1))
                b, _, _ = fill_no(g, what)
                for k in ks:
                    mm = pe.matmul(bank[:, b], w_in[:, k, e * P:(e + 1) * P], xnt[:, k],
                                   start=(k == 0), stop=(k == KD - 1))
                if KD - 1 in ks:
                    mm.then_inc(s_filled, 1)

            def x_proj(g, ks):
                if 0 in ks:
                    take_bank(g, ("xdbl", 0))
                b, _, _ = fill_no(g, ("xdbl", 0))
                wait(pe, s_u, upto(2, after(g), 2 if ks[-1] >= KH else 1))
                for k in ks:
                    mm = pe.matmul(bank[0:XR, b], w_x[:, k], u[1 - g[1]][:, k], start=(k == 0), stop=(k == K - 1))
                if K - 1 in ks:
                    mm.then_inc(s_filled, 1)

            def dt_tile(g, k):
                o = take_bank(g, ("dt", k))
                if k == 0:
                    wait_read(g, ("xdbl", 0))
                pe.matmul(o, w_dt[:, k * P:(k + 1) * P], xdbl[:], start=True, stop=True).then_inc(s_filled, 1)

            def out_tile(g, b, ks):
                if 0 in ks:
                    take_bank(g, ("out", b))
                    if b == 0:
                        wait(pe, s_gated, upto(K, before(g), K))
                bk, _, _ = fill_no(g, ("out", b))
                for k in ks:
                    mm = pe.matmul(bank[:, bk], u[1 - g[1]][:, k, b * T:(b + 1) * T], w_out[:, k],
                                   start=(k == 0), stop=(k == K - 1))
                if K - 1 in ks:
                    mm.then_inc(s_filled, 1)

            def add_states(g, c):
                half, n, kb = c // (4 * N), c // 4 % N, c % 4
                if n == 0:
                    wait(pe, s_y, upto(K, g, KH * half - KH + kb + 1))
                wait(pe, s_hc, upto(UNITS, g, c + 1))
                pe.matmul(y_acc[:, kb], ident[:], hbuf[:, c % NSLOT], start=(n == 0), stop=(n == N - 1)) \
                    .then_inc(s_sum, 1)

            g = (-1, 1)
            pe.wait_ge(s_ident, 2)
            pe.wait_ge(s_wada, 16 * N_ADA_DMAS)
            pe.wait_ge(s_cond, 1)
            for j in range(2 * KD):
                o = take_bank(g, ("ada", j))
                for c in range(KC):
                    mm = pe.matmul(o[:, 0:NSEQ], w_ada[:, c, j * P:(j + 1) * P], cond_s[:, c],
                                   start=(c == 0), stop=(c == KC - 1))
                mm.then_inc(s_filled, 1)
            o = take_bank(g, ("ada", 2 * KD))
            for c in range(KC):
                mm = pe.matmul(o, cond_s[:, c], w_ada[:, c, 2 * D:3 * D], start=(c == 0), stop=(c == KC - 1))
            mm.then_inc(s_filled, 1)
            for k in range(KD):
                turn(g, k)
            pe.wait_ge(s_win, 16)
            for e in range(K):
                project(g, ("conv", e), e, range(KD))
            for e in range(Z_AHEAD):
                project(g, ("z", e), K + e, range(KD))
            pe.wait_ge(s_weights, 16 * N_WEIGHT_DMAS)
            x_proj(g, range(K))
            for k in range(KH):
                dt_tile(g, k)

            def group(g, first, last):
                for h in range(PAIRS):
                    for (kind, t), begin, end in PLAN[h]:
                        if first and kind == "out" or last and is_next((kind, t)):
                            continue
                        if kind == "dt":
                            dt_tile(g, t)
                        elif kind == "z":
                            project(g, (kind, t), K + t, range(begin, end))
                        elif kind == "turn":
                            turn(g, t)
                        elif kind == "out":
                            out_tile(g, t, range(begin, end))
                        elif kind == "conv":
                            project(g, (kind, t), t, range(begin, end))
                        else:
                            x_proj(g, range(begin, end))
                    add_states(g, 2 * h)
                    add_states(g, 2 * h + 1)

            run_groups(pe, group)
            g = (GROUPS // 2, 0)
            for b in range(SEQS):
                out_tile(g, b, range(K))

        @block.scalar
        def _(act):
            def decay_tile(g, c):
                half, n = c // (4 * N), c // 4 % N
                k = half * KH + c % 4
                if n == 0:
                    wait(act, s_dt, upto(2 * K, g, 2 * k + 2))
                wait(act, s_scan, upto(UNITS, g, c - 1))
                nc.scalar.activation(seq3(decay[:, c % 2])[:, :, 1:T], seq3(dt[:, k])[:, :, 1:T], ACT.Exp,
                                     scale=a_neg[:, k, n:n + 1]).then_inc(s_decay, 1)

            def softplus(g, k, r):
                ga = g if k >= KH else after(g)
                b, used, n = fill_no(g, ("dt", k))
                if r == 0:
                    wait(act, s_filled, n + 1)
                    nc.scalar.activation(dt[:, k], bank[:, b], ACT.Abs).then_inc(s_sp, 1)
                if r == 1:
                    wait(act, s_sp, upto(3 * K, ga, 3 * k + 1))
                    nc.scalar.activation(dt[:, k], dt[:, k], ACT.Exp, scale=-1.0).then_inc(s_sp, 1)
                if r == 2:
                    wait(act, s_sp, upto(3 * K, ga, 3 * k + 2))
                    nc.scalar.activation(dt[:, k], dt[:, k], ACT.Ln, bias=1.0).then_inc(s_sp, 1)

            def first_root(g):
                ga = after(g)
                wait(act, s_ln, upto(NORM_STEPS, ga, 2 * SEQS + 1))
                nc.scalar.activation(rstd[:], var_eps[:], ACT.Ln).then_inc(s_rstd, 1)
                wait(act, s_rstd, upto(2, ga, 1))
                nc.scalar.activation(rstd[:], rstd[:], ACT.Exp, scale=-0.5).then_inc(s_rstd, 1)

            def copy_z(g, e):
                b, used, n = fill_no(g, ("z", e))
                wait(act, s_gated, upto(K, g, e + 1 if e < Z_AHEAD else e + 1 - K))
                wait(act, s_filled, n + 1)
                nc.scalar.activation(z[:, e], bank[:, b], ACT.Copy).then_inc(s_free[b], 1)

            def xn_tile(g, k):
                i, p = g
                b, used, n = fill_no(g, ("turn", k))
                wait(act, s_filled, n + 1)
                for j in range(SEQS):
                    col = i * (2 * SEQS) + ((p + 1) * SEQS + j)
                    a = nc.scalar.activation(xnt[:, k, j * T:(j + 1) * T], bank[:, b, j * T:(j + 1) * T],
                                             ACT.Identity, scale=xn_scale[:, k, bass.ds(col, 1)],
                                             bias=xn_shift[:, k, bass.ds(col, 1)])
                a.then_inc(s_free[b], 1)

            def first_tap(g, e):
                b, used, n = fill_no(g, ("conv", e))
                wait(act, s_filled, n + 1)
                nc.scalar.activation(u[1 - g[1]][:, e], bank[:, b], ACT.Identity, scale=conv_k[:, e, DC - 1:DC],
                                     bias=conv_c[:, e:e + 1]).then_inc(s_tap, 1)

            def silu_u(g, half):
                for e in (KH * half + KH - 2, KH * half + KH - 1):
                    b, used, n = fill_no(g, ("conv", e))
                    wait(act, s_free[b], used + 1)
                t = u[1 - g[1]][:, half * KH:half * KH + KH]
                nc.scalar.activation(t, t, ACT.Silu).then_inc(s_u, 1)

            def silu_z(g, half):
                if half == 0:
                    b, used, n = fill_no(g, ("z", K - 1))
                    wait(act, s_free[b], used + 1)
                t = z[:, half * KH:half * KH + KH]
                nc.scalar.activation(t, t, ACT.Silu).then_inc(s_z, 1)

            def copy_xdbl(g):
                b, used, n = fill_no(g, ("xdbl", 0))
                wait(act, s_bcst, upto(16, g, 16))
                wait(act, s_filled, n + 1)
                nc.scalar.activation(xdbl[0:XR, :], bank[0:XR, b], ACT.Copy).then_inc(s_free[b], 1)

            nc.scalar.preload_act_table_set(EXP_TABLES)
            g = (-1, 1)
            first_root(g)
            act.wait_ge(s_wada, 16 * N_ADA_DMAS)
            nc.scalar.activation(cond_s, cond_s, ACT.Silu).then_inc(s_cond, 1)
            act.wait_ge(s_ada, ADA_STEPS)
            for k in range(KD):
                xn_tile(g, k)
            act.wait_ge(s_weights, 16 * N_WEIGHT_DMAS)
            for e in range(K):
                first_tap(g, e)
            for e in range(Z_AHEAD):
                copy_z(g, e)
            silu_u(g, 0)
            silu_u(g, 1)
            copy_xdbl(g)
            nc.scalar.preload_act_table_set(EXP_TABLES)
            nc.scalar.activation(a_neg[:], a_neg[:], ACT.Exp).then_inc(s_cond, 1)
            for k in range(KH):
                for r in range(3):
                    softplus(g, k, r)
            act.wait_ge(s_set, 6)

            def group(g, first, last):
                for h in range(PAIRS):
                    if h == SILU_U and not last:
                        silu_u(g, 0)
                        silu_u(g, 1)
                        nc.scalar.preload_act_table_set(EXP_TABLES)
                    if h == SILU_Z:
                        silu_z(g, 0)
                        silu_z(g, 1)
                        nc.scalar.preload_act_table_set(EXP_TABLES)
                    decay_tile(g, 2 * h)
                    for gd, k in due(g, h, first, last, "dt", 3, 2):
                        softplus(gd, k, 2)
                    for gd, k in due(g, h, first, last, "dt", 2, 1):
                        softplus(gd, k, 0)
                    for gd, e in due(g, h, first, last, "z", 2):
                        copy_z(gd, e)
                    if h == AT_TURN - 6 and not last:
                        first_root(g)
                    for gd, k in due(g, h, first, last, "turn", 2):
                        xn_tile(gd, k)
                    for gd, e in due(g, h, first, last, "conv", 2):
                        first_tap(gd, e)
                    for gd, _ in due(g, h, first, last, "xdbl", 1):
                        copy_xdbl(gd)
                    decay_tile(g, 2 * h + 1)
                    for gd, k in due(g, h, first, last, "dt", 2, 1):
                        softplus(gd, k, 1)

            run_groups(act, group)

        @block.vector
        def _(dve):
            def statistics(g, b):
                if b == 0:
                    wait(dve, s_x, upto(16, after(g), 16))
                dve.bn_stats(stats[:, b], xs[:, b]).then_inc(s_ln, 1)

            def statistics_made(g):
                wait(dve, s_ln, upto(NORM_STEPS, after(g), SEQS))

            def aggregate(g):
                for b in range(SEQS):
                    dve.bn_aggr(moments[:, b], stats[:, b]).then_inc(s_ln, 1)
                wait(dve, s_ln, upto(NORM_STEPS, after(g), 2 * SEQS))
                dve.tensor_scalar(var_eps[:], moments[:, :, 1], EPS, None, ALU.add).then_inc(s_ln, 1)

            def root(g):
                ga = after(g)
                at = 2 * SEQS + 1
                wait(dve, s_rstd, upto(2, ga, 2))
                dve.tensor_tensor(newton[:], rstd[:], rstd[:], ALU.mult).then_inc(s_ln, 1)
                wait(dve, s_ln, upto(NORM_STEPS, ga, at + 1))
                dve.tensor_tensor(newton[:], newton[:], var_eps[:], ALU.mult).then_inc(s_ln, 1)
                wait(dve, s_ln, upto(NORM_STEPS, ga, at + 2))
                dve.tensor_scalar(newton[:], newton[:], -0.5, 1.5, ALU.mult, ALU.add).then_inc(s_ln, 1)
                wait(dve, s_ln, upto(NORM_STEPS, ga, at + 3))
                dve.tensor_tensor(rstd[:], rstd[:], newton[:], ALU.mult).then_inc(s_ln, 1)

            def normalise(g, b):
                if b == 0:
                    wait(dve, s_ln, upto(NORM_STEPS, after(g), 2 * SEQS + 5))
                dve.tensor_scalar(xs[:, b], xs[:, b], moments[:, b, 0:1], rstd[:, b:b + 1],
                                  ALU.subtract, ALU.mult).then_inc(s_ln, 1)

            def tap(g, e, j):
                b, used, n = fill_no(g, ("conv", e))
                back = j + 1
                if j == 0:
                    wait(dve, s_tap, upto(K, after(g), e + 1))
                else:
                    wait(dve, s_conv, upto(2 * K, after(g), 2 * e + j))
                acc = seq3(u[1 - g[1]][:, e])[:, :, back:T]
                t = dve.scalar_tensor_tensor(acc, seq3(bank[:, b])[:, :, 0:T - back],
                                             conv_k[:, e, DC - 1 - back:DC - back], acc, ALU.mult, ALU.add)
                if back < DC - 1:
                    t.then_inc(s_conv, 1)
                else:
                    t.then_inc(s_free[b], 1)

            def finish_dt(g, k, r):
                ga = g if k >= KH else after(g)
                b, used, n = fill_no(g, ("dt", k))
                if r == 0:
                    wait(dve, s_sp, upto(3 * K, ga, 3 * k + 3))
                    dve.scalar_tensor_tensor(dt[:, k], bank[:, b], 0.0, dt[:, k], ALU.max, ALU.add) \
                        .then_inc(s_free[b], 1)
                else:
                    wait(dve, s_free[b], used + 1)
                    if k == 0:
                        wait(dve, s_u, upto(2, ga, 2))
                    dve.tensor_tensor(v[:, k], dt[:, k], u[ga[1]][:, k], ALU.mult).then_inc(s_dt, 2)

            def drive(g, h):
                if h == PAIRS:
                    g, h = after(g), 0
                s = h // 2
                half, n = s // N, s % N
                k = half * KH + 2 * (h % 2)
                if n == 0:
                    wait(dve, s_dt, upto(2 * K, g, 2 * (k + 2)))
                wait(dve, s_sum, upto(UNITS, g, 2 * h + 2 - NSLOT))
                if h % 2 == 0:
                    wait(dve, s_bc[s % NBC], upto(16 * (STEPS // NBC), g, 16 * (s // NBC + 1)))
                at = 2 * h % NSLOT
                dve.tensor_tensor(hbuf[:, at:at + 2], v[:, k:k + 2],
                                  bc[:, s % NBC, 0].unsqueeze(1).broadcast_to([P, 2, TOK]), ALU.mult) \
                    .then_inc(s_drive, 1)

            def scan(g, c):
                t = hbuf[:, c % NSLOT]
                if c % 2 == 0:
                    wait(dve, s_drive, upto(PAIRS, g, c // 2 + 1))
                wait(dve, s_decay, upto(UNITS, g, c + 1))
                dve.tensor_tensor_scan(t, decay[:, c % 2], t, 0.0, ALU.mult, ALU.add).then_inc(s_scan, 1)

            def take_y(g, half, kb):
                k = half * KH + kb
                wait(dve, s_sum, upto(UNITS, g, 4 * (half * N + N - 1) + kb + 1))
                dve.scalar_tensor_tensor(u[g[1]][:, k], u[g[1]][:, k], d_skip[:, k:k + 1], y_acc[:, kb],
                                         ALU.mult, ALU.add).then_inc(s_y, 1)

            def gate_out(g, b):
                bk, used, n = fill_no(g, ("out", b))
                if b == 0:
                    wait(dve, s_res, upto(32, before(g), 32))
                wait(dve, s_filled, n + 1)
                dve.tensor_tensor(gate_bc[:, b], bank[:, bk], gate_bc[:, b], ALU.mult).then_inc(s_free[bk], 1)

            dve.memset(w_dt[:], 0.0).then_inc(s_set, 1)
            dve.memset(xdbl[:], 0.0).then_inc(s_set, 1)
            dve.wait_ge(s_set, 2)
            dve.memset(xdbl[XR:XR + 1, :], 1.0).then_inc(s_set, 1)
            dve.memset(decay[:], 0.0).then_inc(s_set, 1)
            g = (-1, 1)
            for b in range(SEQS):
                statistics(g, b)
            statistics_made(g)
            aggregate(g)
            root(g)
            for b in range(SEQS):
                normalise(g, b)
            dve.wait_ge(s_wada, 16 * N_ADA_DMAS)
            done = 0
            dve.tensor_scalar(ada_bias[:, KD:2 * KD], ada_bias[:, KD:2 * KD], 1.0, None, ALU.add).then_inc(s_ada, 1)
            done += 1
            dve.wait_ge(s_ada, done)
            for k in range(KD):
                b, used, n = fill_no(g, ("ada", k))
                dve.wait_ge(s_filled, n + 1)
                dve.tensor_scalar(xn_shift[:, k], bank[:, b, 0:NSEQ], ada_bias[:, k:k + 1], None, ALU.add).then_inc(s_ada, 1)
                done += 1
                dve.wait_ge(s_ada, done)
                dve.sem_inc(s_free[b], 1)
            for k in range(KD):
                b, used, n = fill_no(g, ("ada", KD + k))
                dve.wait_ge(s_filled, n + 1)
                dve.tensor_scalar(one_scale[:, k], bank[:, b, 0:NSEQ], ada_bias[:, KD + k:KD + k + 1], None,
                                  ALU.add).then_inc(s_ada, 1)
                done += 1
                dve.wait_ge(s_ada, done)
                dve.sem_inc(s_free[b], 1)
                dve.tensor_scalar(xn_scale[:, k], one_scale[:, k], ln_gain[:, k:k + 1], None, ALU.mult).then_inc(s_ada, 1)
                dve.scalar_tensor_tensor(xn_shift[:, k], one_scale[:, k], ln_bias[:, k:k + 1], xn_shift[:, k],
                                         ALU.mult, ALU.add).then_inc(s_ada, 1)
                done += 2
            b, used, n = fill_no(g, ("ada", 2 * KD))
            dve.wait_ge(s_filled, n + 1)
            dve.tensor_tensor(gate_rows, bank[:, b], gate_bias, ALU.add).then_inc(s_ada, 1)
            done += 1
            dve.wait_ge(s_ada, done)
            assert done == ADA_STEPS
            dve.sem_inc(s_free[b], 1)
            dve.wait_ge(s_weights, 16 * N_WEIGHT_DMAS)
            for e in range(K):
                for j in range(3):
                    tap(g, e, j)
            dve.wait_ge(s_cond, 2)
            dve.tensor_scalar(a_neg[:], a_neg[:], -1.0, None, ALU.mult).then_inc(s_set, 2)
            dve.wait_ge(s_gate_st, 16)
            for k in range(KH):
                finish_dt(g, k, 0)
                finish_dt(g, k, 1)
            drive((0, 0), 0)

            def group(g, first, last):
                for h in range(PAIRS):
                    scan(g, 2 * h)
                    for gd, k in due(g, h, first, last, "dt", 4, 3):
                        finish_dt(gd, k, 0)
                    for gd, k in due(g, h, first, last, "dt", -1000, 3):
                        finish_dt(gd, k, 1)
                    for gd, e in due(g, h, first, last, "conv", 2):
                        tap(gd, e, 0)
                    for gd, e in due(g, h, first, last, "conv", 3):
                        tap(gd, e, 2)
                    if h < PAIRS - 1 or not last:
                        drive(g, h + 1)
                    if h == AT_TURN - 7 and not last:
                        statistics_made(g)
                    scan(g, 2 * h + 1)
                    for gd, k in due(g, h, first, last, "dt", 4, 1000):
                        finish_dt(gd, k, 1)
                    for gd, b in due(g, h, first, last, "out", 2):
                        gate_out(gd, b)
                    for gd, e in due(g, h, first, last, "conv", 2):
                        tap(gd, e, 1)
                    if not last:
                        if AT_TURN - 12 <= h < AT_TURN - 12 + SEQS:
                            statistics(g, h - (AT_TURN - 12))
                        if h == AT_TURN - 7:
                            aggregate(g)
                        if h == AT_TURN - 5:
                            root(g)
                        if AT_TURN - 4 <= h < AT_TURN:
                            normalise(g, h - (AT_TURN - 4))
                    if h == 1 and not first:
                        for kb in range(KH):
                            take_y(before(g), 1, kb)
                    if h == 2 * N + 1:
                        for kb in range(KH):
                            take_y(g, 0, kb)

            run_groups(dve, group)
            g = (GROUPS // 2, 0)
            for kb in range(KH):
                take_y(before(g), 1, kb)
            for b in range(SEQS):
                gate_out(g, b)

        @block.gpsimd
        def _(pool):
            def weigh(g, c):
                s = c // 4
                wait(pool, s_scan, upto(UNITS, g, c + 1))
                if c % 4 == 0:
                    wait(pool, s_bc[s % NBC], upto(16 * (STEPS // NBC), g, 16 * (s // NBC + 1)))
                nc.gpsimd.tensor_tensor(hbuf[:, c % NSLOT], hbuf[:, c % NSLOT], bc[:, s % NBC, 1],
                                        ALU.mult).then_inc(s_hc, 1)

            def gate_y(g, k):
                wait(pool, s_y, upto(K, g, k + 1))
                wait(pool, s_z, upto(2, g, k // KH + 1))
                nc.gpsimd.tensor_tensor(u[g[1]][:, k], u[g[1]][:, k], z[:, k], ALU.mult).then_inc(s_gated, 1)

            def add_residual(g, b):
                bk, used, n = fill_no(g, ("out", b))
                wait(pool, s_free[bk], used + 1)
                nc.gpsimd.tensor_tensor(x_res[:, b], x_res[:, b], gate_bc[:, b], ALU.add).then_inc(s_oadd, 1)

            pool.memset(ident[:], 0.0).then_inc(s_ident, 1)
            pool.wait_ge(s_ident, 1)
            pool.affine_select(out=ident[:], in_=ident[:], compare_op=ALU.not_equal, fill=1.0, base=0,
                               pattern=[[-1, P]], channel_multiplier=1).then_inc(s_ident, 1)

            def group(g, first, last):
                for h in range(PAIRS):
                    weigh(g, 2 * h)
                    if 2 <= h < 2 + KH and not first:
                        gate_y(before(g), KH + h - 2)
                    if 2 * N + 4 <= h < 2 * N + 4 + KH:
                        gate_y(g, h - 2 * N - 4)
                    weigh(g, 2 * h + 1)
                    for gd, b in due(g, h, first, last, "out", 3):
                        add_residual(gd, b)

            run_groups(pool, group)
            g = (GROUPS // 2, 0)
            for k in range(KH, K):
                gate_y(before(g), k)
            for b in range(SEQS):
                add_residual(g, b)


def kernel(**inputs):
    import numpy as _np
    import concourse.bacc as _bacc
    from concourse.bass_utils import run_bass_kernel_spmd as _run

    w = {k.replace("L0_cond_", ""): _np.asarray(a) for k, a in inputs.items()}

    def by_channel(a):
        return a.reshape(-1, P).T

    laid = {
        "x": w["x"], "cond_t": w["cond_2048"].T, "ln_g": by_channel(w["ln_g"]), "ln_b": by_channel(w["ln_b"]),
        "ada_wt": w["ada_w"].T, "ada_b": by_channel(w["ada_b"]), "gate_b": w["ada_b"][-w["ln_g"].size:], "in_proj_wt": w["in_proj_w"].T,
        "conv_w": w["conv_w"], "conv_b": by_channel(w["conv_b"]), "x_proj_wt": w["x_proj_w"].T,
        "dt_proj_wt": w["dt_proj_w"].T, "dt_proj_b": w["dt_proj_b"].reshape(1, -1),
        "a_log": w["A_log"], "d_param": by_channel(w["D_param"]), "out_proj_wt": w["out_proj_w"].T,
    }
    nc = _bacc.Bacc("TRN2", target_bir_lowering=False, num_devices=1)
    arrays, args = {}, []
    for name, a in laid.items():
        a = _np.ascontiguousarray(a)
        arrays[f"in_{name}"] = a
        args.append(nc.dram_tensor(f"in_{name}", a.shape, mybir.dt.from_np(a.dtype), kind="ExternalInput").ap())
    args.append(nc.dram_tensor("out_0", w["x"].shape, F32, kind="ExternalOutput").ap())
    mamba_program(nc, *args)
    r = _run(nc, [arrays], core_ids=[0])
    return r.results[0]["out_0"]
```

```python
from contextlib import ExitStack

import concourse.bass as bass
from concourse import mybir

P = 128
F32 = mybir.dt.float32
ALU = mybir.AluOpType
ACT = mybir.ActivationFunctionType
EPS = 1e-5

SEQS = 4
NSLOT = 8
NBC = 4
EXP_TABLES = "natural_log_exp_and_others"


def mamba_program(nc, x, cond_t, ln_g, ln_b, ada_wt, ada_b, gate_b, in_proj_wt, conv_w, conv_b, x_proj_wt,
                  dt_proj_wt, dt_proj_b, a_log, d_param, out_proj_wt, out):
    NSEQ, T, D = x.shape
    DI = conv_w.shape[0]
    N = a_log.shape[1]
    R = dt_proj_wt.shape[0]
    DC = conv_w.shape[1]
    COND = cond_t.shape[0]
    E3 = ada_wt.shape[1]
    TOK = SEQS * T
    GROUPS = NSEQ // SEQS
    KD, K, KC = D // P, DI // P, COND // P
    KH = K // 2
    STEPS = 2 * N
    PAIRS = 2 * STEPS
    UNITS = 2 * PAIRS
    XR = R + 2 * N
    assert T == P and TOK == 512 and D == 512 and K == 8 and N == 16 and XR < P and GROUPS % 2 == 0

    Z_AHEAD = 4
    PRODUCTS = {"z": KD, "z0": KD, "gate": KC, "conv": KD, "out": K, "xdbl": K, "dt": 1, "turn": 1}
    PLAN = {h: [] for h in range(PAIRS)}
    END = {}

    def lay(fills, begin, end):
        products = [(f, j) for f in fills for j in range(PRODUCTS[f[0]])]
        for n, (f, j) in enumerate(products):
            h = begin + n * (end - begin) // len(products)
            if PLAN[h] and PLAN[h][-1][0] == f:
                PLAN[h][-1] = (f, PLAN[h][-1][1], j + 1)
            else:
                PLAN[h].append((f, j, j + 1))
            END[f] = h
        return fills

    AT_TURN = 20
    FILLS = lay([("z", 4), ("dt", 4), ("z", 5), ("dt", 5), ("z", 6), ("dt", 6), ("z", 7), ("dt", 7)], 0, 10)
    FIRST = list(FILLS)
    FILLS += lay([("out", b) for b in range(SEQS - 1)], 10, AT_TURN)
    FIRST += lay([("z0", 1), ("z0", 2), ("z0", 3)], 10, AT_TURN)
    NEXT = lay([("turn", k) for k in range(KD)], AT_TURN, 23)
    FILLS += NEXT + lay([("out", SEQS - 1)], 23, 27)
    FIRST += NEXT + lay([("gate", 0)], 23, 27)
    LAST = [f for f in FILLS if f not in NEXT]
    NEXT += lay([("conv", e) for e in range(KH)], 27, 36)
    NEXT += lay([("z", 0), ("conv", 4), ("conv", 5), ("z", 1), ("conv", 6), ("conv", 7)], 36, 50)
    NEXT += lay([("z", 2)], 50, 52)
    NEXT += lay([("xdbl", 0)], 53, 56)
    NEXT += lay([("dt", k) for k in range(KH)], 57, 57 + KH)
    NEXT += lay([("z", 3)], 61, 63)
    FIRST += NEXT[KD:]
    FILLS += NEXT[KD:]
    SILU_U, SILU_Z = 53, END["z", K - 1] + 4

    def is_next(f):
        return f in NEXT

    def left_out(f, first, last):
        if f[0] in ("z0", "gate"):
            return not first
        return first and f[0] == "out" or last and is_next(f)

    SETUP = [("ada", j) for j in range(2 * KD)]
    SETUP += [("turn", k) for k in range(KD)] + [("conv", e) for e in range(K)]
    SETUP += [("z", 0), ("xdbl", 0)] + [("dt", k) for k in range(KH)]
    TAIL = [("out", b) for b in range(SEQS)]

    def due(g, h, first, last, kind, lag):
        for f in FIRST if first else FILLS:
            if f[0] == kind:
                at = END[f] + lag
                if at == h and not left_out(f, first, last):
                    yield g, f[1]
                if at == h + PAIRS and not first:
                    yield before(g), f[1]

    def before(g):
        i, p = g
        return (i, p - 1) if p else (i - 1, 1)

    def after(g):
        i, p = g
        return (i + 1, 0) if p else (i, 1)

    def upto(per_group, g, extra=0):
        i, p = g
        return i * (2 * per_group) + (per_group * p + extra)

    def fill_no(g, what):
        i, p = g
        nf = len(FILLS)
        if isinstance(i, int) and i == -1:
            n = SETUP.index(what)
        elif (isinstance(i, int) and 2 * i + p == 0):
            n = len(SETUP) + FIRST.index(what)
        elif isinstance(i, int) and 2 * i + p >= GROUPS - 1:
            n = len(SETUP) + len(FIRST) + nf * (GROUPS - 2)
            n += LAST.index(what) if 2 * i + p < GROUPS else len(LAST) + TAIL.index(what)
        else:
            at = len(SETUP) + len(FIRST) + nf * (p - 1) + FILLS.index(what)
            return at % 2, i * nf + at // 2, i * (2 * nf) + at
        return n % 2, n // 2, n

    def wait(eng, sem, value):
        if isinstance(value, int) and value <= 0:
            return
        eng.wait_ge(sem, value)

    with ExitStack() as ctx:
        def sb(name, shape):
            return ctx.enter_context(nc.sbuf_tensor(name, shape, F32))

        def ps(name, shape):
            return ctx.enter_context(nc.psum_tensor(name, shape, F32))

        def sem(name):
            return ctx.enter_context(nc.semaphore(name))

        w_in = sb("w_in", [P, KD, 2 * DI])
        w_out = sb("w_out", [P, K, D])
        w_x = sb("w_x", [P, K, XR])
        w_dt = sb("w_dt", [P, DI])
        ident = sb("ident", [P, P])
        a_neg = sb("a_neg", [P, K, N])
        d_skip = sb("d_skip", [P, K])
        conv_k = sb("conv_k", [P, K, DC])
        conv_c = sb("conv_c", [P, K])
        ln_gain = sb("ln_gain", [P, KD])
        ln_bias = sb("ln_bias", [P, KD])
        ada_bias = sb("ada_bias", [P, E3 // P])
        xn_scale = sb("xn_scale", [P, KD, NSEQ])
        xn_shift = sb("xn_shift", [P, KD, NSEQ])
        act_mem = sb("act_mem", [P, 3, K, TOK])
        u = [act_mem[:, 0], act_mem[:, 1]]
        z = act_mem[:, 2]
        xs = sb("xs", [P, SEQS, D])
        xnt = sb("xnt", [P, KD, TOK])
        xdbl = sb("xdbl", [P, TOK])
        dt = sb("dt", [P, K, TOK])
        v = sb("v", [P, K, TOK])
        hbuf = sb("hbuf", [P, NSLOT, TOK])
        bc = sb("bc", [P, NBC, 2, TOK])
        gate_bc = sb("gate_bc", [P, SEQS, D])
        x_res = sb("x_res", [P, SEQS, D])
        stats = sb("stats", [P, SEQS, 6])
        moments = sb("moments", [P, SEQS, 2])
        var_eps = sb("var_eps", [P, SEQS])
        rstd = sb("rstd", [P, SEQS])
        newton = sb("newton", [P, SEQS])
        w_ada = [m.rearrange("p k t -> p (k t)").rearrange("p (c e) -> p c e", c=KC) for m in (z, u[0], u[1])]
        cond_s = x_res[:, 2:4, :].rearrange("p k t -> p (k t)").rearrange("p (c b) -> p c b", c=KC)
        one_scale = v[:, 0, :].rearrange("p (k b) -> p k b", k=KD)
        gate_rows = x_res[:, 0]
        gate_bias = x_res[:, 1]

        y_acc = ps("y_acc", [P, KH, TOK])
        decay = ps("decay", [P, 2, TOK])
        bank = ps("bank", [P, 2, TOK])

        gate_dram = nc.dram_tensor("gate_rows_dram", (NSEQ, D), F32, kind="Internal").ap()
        bc_dram = nc.dram_tensor("bc_dram", (2, 2 * N, TOK), F32, kind="Internal").ap()

        s_small = sem("vectors_loaded")
        s_wada = [sem(f"ada_weights_{part}_loaded") for part in ("shift", "scale", "gate")]
        s_win = [sem(f"w_in_{part}_loaded") for part in ("x", "z")]
        s_wx = sem("w_x_and_w_dt_loaded")
        s_wout = sem("w_out_loaded")
        s_ident = sem("identity_made")
        s_set = sem("constants_set")
        s_cond = sem("cond_silu_made")
        s_ada = sem("ada_steps")
        s_gate_st = sem("gate_rows_stored")
        s_x = sem("x_loaded")
        s_ln = sem("norm_steps")
        s_rstd = sem("rstd_steps")
        s_filled = sem("bank_filled")
        s_free = [sem("bank0_free"), sem("bank1_free")]
        s_tap = sem("first_tap_made")
        s_conv = sem("conv_taps")
        s_u = sem("u_made")
        s_bcst = sem("bc_stored")
        s_bc = [sem(f"bc{j}_loaded") for j in range(NBC)]
        s_sp = sem("softplus_steps")
        s_dt = sem("dt_and_v_made")
        s_decay = sem("decays_made")
        s_drive = sem("drives_made")
        s_scan = sem("scans_done")
        s_hc = sem("hc_made")
        s_sum = sem("units_summed")
        s_y = sem("y_made")
        s_z = sem("silu_z_made")
        s_gated = sem("y_gated")
        s_res = sem("residual_loaded")
        s_oadd = sem("outputs_added")
        s_out = sem("out_stored")

        x_tok = x.rearrange("(g b) t d -> g t b d", b=SEQS)
        out_tok = out.rearrange("(g b) t d -> g t b d", b=SEQS)
        gate_g = gate_dram.rearrange("(g b) d -> g b d", b=SEQS)

        N_SMALL = 9
        ADA_STEPS = 4 * KD + 1
        NORM_STEPS = 3 * SEQS + 5

        def seq3(ap):
            return ap.rearrange("p (b t) -> p b t", b=SEQS)

        block = ctx.enter_context(nc.Block())

        def store_bc(sp, g):
            i, p = g
            b, used, n = fill_no(g, ("xdbl", 0))
            wait(sp, s_free[b], used + 1)
            sp.dma_start(bc_dram[1 - p], xdbl[R:XR, :]).then_inc(s_bcst, 16)

        def load_bc(sp, g, s):
            i, p = g
            n = s % N
            par = p if s < STEPS else 1 - p
            if s == STEPS:
                wait(sp, s_bcst, upto(16, g, 32))
            else:
                wait(sp, s_hc, upto(UNITS, g, 4 * (s - NBC) + 4))
            sp.dma_start(bc[:, s % NBC], bc_dram[par, n:2 * N:N].partition_broadcast(P)) \
                .then_inc(s_bc[s % NBC], 16)

        def load_residual(sp, g):
            i, p = g
            wait(sp, s_out, upto(16, g))
            sp.dma_start(x_res[:], x_tok[2 * i + p]).then_inc(s_res, 16)
            wait(sp, s_hc, upto(UNITS, g, 4 * (STEPS - NBC) + 4))
            sp.dma_start(gate_bc[:], gate_g[2 * i + p].partition_broadcast(P)).then_inc(s_res, 16)

        def store_out(sp, g):
            i, p = g
            wait(sp, s_oadd, upto(SEQS, g, SEQS))
            sp.dma_start(out_tok[2 * i + p], x_res[:]).then_inc(s_out, 16)

        def run_groups(eng, group):
            group((0, 0), True, False)
            group((0, 1), False, False)
            with eng.Fori(1, GROUPS // 2 - 1) as i:
                group((i, 0), False, False)
                group((i, 1), False, False)
            group((GROUPS // 2 - 1, 0), False, False)
            group((GROUPS // 2 - 1, 1), False, True)

        @block.sync
        def _(sp):
            for dst, src in (
                (cond_s, cond_t.rearrange("(c p) b -> p c b", p=P)),
                (ada_bias[:], ada_b),
                (ln_gain[:], ln_g),
                (ln_bias[:], ln_b),
                (a_neg[:], a_log.rearrange("(k p) n -> p k n", p=P)),
                (conv_k[:], conv_w.rearrange("(k p) j -> p k j", p=P)),
                (conv_c[:], conv_b),
                (d_skip[:], d_param),
                (gate_bias, gate_b.partition_broadcast(P)),
            ):
                sp.dma_start(dst, src).then_inc(s_small, 16)
            ada_parts = ada_wt.rearrange("(c p) (q e) -> q p c e", p=P, q=3)
            in_parts = in_proj_wt.rearrange("(k p) (q e) -> q p k e", p=P, q=2)
            for q in range(2):
                sp.dma_start(w_ada[q], ada_parts[q]).then_inc(s_wada[q], 16)
                if q == 0:
                    sp.dma_start(xs[:], x_tok[0]).then_inc(s_x, 16)
            sp.dma_start(w_in[:, :, 0:DI], in_parts[0]).then_inc(s_win[0], 16)
            sp.dma_start(w_x[:], x_proj_wt.rearrange("(k p) e -> p k e", p=P)).then_inc(s_wx, 16)
            sp.wait_ge(s_set, 4)
            sp.dma_start(w_dt[0:R, :], dt_proj_wt).then_inc(s_wx, 16)
            sp.dma_start(w_dt[XR:XR + 1, :], dt_proj_b).then_inc(s_wx, 16)
            sp.dma_start(w_in[:, :, DI:], in_parts[1]).then_inc(s_win[1], 16)
            sp.dma_start(w_ada[2], ada_parts[2]).then_inc(s_wada[2], 16)
            sp.dma_start(w_out[:], out_proj_wt.rearrange("(k p) e -> p k e", p=P)).then_inc(s_wout, 16)
            store_bc(sp, (-1, 1))
            sp.wait_ge(s_bcst, 16)
            for s in range(NBC):
                load_bc(sp, (0, 0), s)
            sp.dma_start(xs[:], x_tok[1]).then_inc(s_x, 16)

            def group(g, first, last):
                i, p = g
                for s in range(STEPS):
                    if not first and s == 16:
                        store_out(sp, before(g))
                    if not last and s == 16 and (not isinstance(i, int) or 2 * i + p + 2 < GROUPS):
                        load_x(sp, g)
                    if not last and s == STEPS - NBC:
                        store_bc(sp, g)
                    if first and s == STEPS // 2:
                        b, used, _ = fill_no(g, ("gate", 0))
                        wait(sp, s_free[b], used + 1)
                        sp.dma_start(gate_dram, gate_rows).then_inc(s_gate_st, 16)
                    if first and s == STEPS - NBC:
                        sp.wait_ge(s_gate_st, 16)
                    if s == STEPS - NBC:
                        load_residual(sp, g)
                    if s < STEPS - NBC or not last:
                        load_bc(sp, g, s + NBC)

            def load_x(sp, g):
                i, p = g
                wait(sp, s_filled, fill_no(g, ("turn", KD - 1))[2] + 1)
                sp.dma_start(xs[:], x_tok[2 * i + p + 2]).then_inc(s_x, 16)

            run_groups(sp, group)
            store_out(sp, (GROUPS // 2 - 1, 1))
            sp.wait_ge(s_out, 16 * GROUPS)

        @block.tensor
        def _(pe):
            def take_bank(g, what):
                b, used, _ = fill_no(g, what)
                wait(pe, s_free[b], used)
                return bank[:, b]

            def wait_read(g, what):
                b, used, _ = fill_no(g, what)
                wait(pe, s_free[b], used + 1)

            def turn(g, k):
                o = take_bank(g, ("turn", k))
                if k == 0:
                    wait(pe, s_ln, upto(NORM_STEPS, after(g), NORM_STEPS))
                for b in range(SEQS):
                    mm = pe.transpose(o[:, b * T:(b + 1) * T], xs[:, b, k * P:(k + 1) * P], ident[:])
                mm.then_inc(s_filled, 1)

            def project(g, what, e, ks):
                if 0 in ks:
                    take_bank(g, what)
                b, _, _ = fill_no(g, what)
                for k in ks:
                    if what == ("conv", 0):
                        wait_read(g, ("turn", k))
                    mm = pe.matmul(bank[:, b], w_in[:, k, e * P:(e + 1) * P], xnt[:, k],
                                   start=(k == 0), stop=(k == KD - 1))
                if KD - 1 in ks:
                    mm.then_inc(s_filled, 1)

            def x_proj(g, ks):
                if 0 in ks:
                    take_bank(g, ("xdbl", 0))
                b, _, _ = fill_no(g, ("xdbl", 0))
                wait(pe, s_u, upto(2, after(g), 2 if ks[-1] >= KH else 1))
                for k in ks:
                    mm = pe.matmul(bank[0:XR, b], w_x[:, k], u[1 - g[1]][:, k], start=(k == 0), stop=(k == K - 1))
                if K - 1 in ks:
                    mm.then_inc(s_filled, 1)

            def dt_tile(g, k):
                o = take_bank(g, ("dt", k))
                if k == 0:
                    wait_read(g, ("xdbl", 0))
                pe.matmul(o, w_dt[:, k * P:(k + 1) * P], xdbl[:], start=True, stop=True).then_inc(s_filled, 1)

            def out_tile(g, b, ks):
                if 0 in ks:
                    take_bank(g, ("out", b))
                    if b == 0:
                        wait(pe, s_gated, upto(K, before(g), K))
                bk, _, _ = fill_no(g, ("out", b))
                for k in ks:
                    mm = pe.matmul(bank[:, bk], u[1 - g[1]][:, k, b * T:(b + 1) * T], w_out[:, k],
                                   start=(k == 0), stop=(k == K - 1))
                if K - 1 in ks:
                    mm.then_inc(s_filled, 1)

            def add_states(g, c):
                half, n, kb = c // (4 * N), c // 4 % N, c % 4
                if n == 0:
                    wait(pe, s_y, upto(K, g, KH * half - KH + kb + 1))
                wait(pe, s_hc, upto(UNITS, g, c + 1))
                pe.matmul(y_acc[:, kb], ident[:], hbuf[:, c % NSLOT], start=(n == 0), stop=(n == N - 1)) \
                    .then_inc(s_sum, 1)

            g = (-1, 1)
            pe.wait_ge(s_ident, 2)
            pe.wait_ge(s_cond, 2)
            for j in range(2 * KD):
                if j % KD == 0:
                    pe.wait_ge(s_wada[j // KD], 16)
                o = take_bank(g, ("ada", j))
                for c in range(KC):
                    mm = pe.matmul(o[:, 0:NSEQ], w_ada[j // KD][:, c, j % KD * P:(j % KD + 1) * P], cond_s[:, c],
                                   start=(c == 0), stop=(c == KC - 1))
                mm.then_inc(s_filled, 1)
            for k in range(KD):
                turn(g, k)
            pe.wait_ge(s_win[0], 16)
            for e in range(K):
                project(g, ("conv", e), e, range(KD))
            pe.wait_ge(s_win[1], 16)
            project(g, ("z", 0), K, range(KD))
            pe.wait_ge(s_wx, 16 * 3)
            x_proj(g, range(KH))
            x_proj(g, range(KH, K))
            for k in range(KH):
                dt_tile(g, k)

            def gate_product(g, cs):
                b, _, _ = fill_no(g, ("gate", 0))
                if 0 in cs:
                    take_bank(g, ("gate", 0))
                    pe.wait_ge(s_wada[2], 16)
                for c in cs:
                    mm = pe.matmul(bank[:, b], cond_s[:, c], w_ada[2][:, c], start=(c == 0), stop=(c == KC - 1))
                if KC - 1 in cs:
                    mm.then_inc(s_filled, 1)

            def group(g, first, last):
                for h in range(PAIRS):
                    for (kind, t), begin, end in PLAN[h]:
                        if left_out((kind, t), first, last):
                            continue
                        if kind == "dt":
                            dt_tile(g, t)
                        elif kind in ("z", "z0"):
                            project(g, (kind, t), K + t, range(begin, end))
                        elif kind == "gate":
                            gate_product(g, range(begin, end))
                        elif kind == "turn":
                            turn(g, t)
                        elif kind == "out":
                            out_tile(g, t, range(begin, end))
                        elif kind == "conv":
                            project(g, (kind, t), t, range(begin, end))
                        else:
                            x_proj(g, range(begin, end))
                    if first and h == PAIRS - 1:
                        pe.wait_ge(s_wout, 16)
                    add_states(g, 2 * h)
                    add_states(g, 2 * h + 1)

            run_groups(pe, group)
            g = (GROUPS // 2, 0)
            for b in range(SEQS):
                out_tile(g, b, range(K))

        @block.scalar
        def _(act):
            def decay_tile(g, c):
                half, n = c // (4 * N), c // 4 % N
                k = half * KH + c % 4
                if n == 0:
                    wait(act, s_dt, upto(2 * K, g, 2 * k + 2))
                wait(act, s_scan, upto(UNITS, g, c - 1))
                nc.scalar.activation(seq3(decay[:, c % 2])[:, :, 1:T], seq3(dt[:, k])[:, :, 1:T], ACT.Exp,
                                     scale=a_neg[:, k, n:n + 1]).then_inc(s_decay, 1)

            def softplus(g, k, r):
                ga = g if k >= KH else after(g)
                b, used, n = fill_no(g, ("dt", k))
                if r == 0:
                    wait(act, s_filled, n + 1)
                    nc.scalar.activation(dt[:, k], bank[:, b], ACT.Abs).then_inc(s_sp, 1)
                    if k < KH:
                        nc.scalar.activation(v[:, k], bank[:, b], ACT.Relu).then_inc(s_free[b], 1)
                if r == 1:
                    wait(act, s_sp, upto(3 * K, ga, 3 * k + 1))
                    nc.scalar.activation(dt[:, k], dt[:, k], ACT.Exp, scale=-1.0).then_inc(s_sp, 1)
                if r == 2:
                    wait(act, s_sp, upto(3 * K, ga, 3 * k + 2))
                    nc.scalar.activation(dt[:, k], dt[:, k], ACT.Ln, bias=1.0).then_inc(s_sp, 1)

            def first_root(g):
                ga = after(g)
                wait(act, s_ln, upto(NORM_STEPS, ga, 2 * SEQS + 1))
                nc.scalar.activation(rstd[:], var_eps[:], ACT.Ln).then_inc(s_rstd, 1)
                wait(act, s_rstd, upto(2, ga, 1))
                nc.scalar.activation(rstd[:], rstd[:], ACT.Exp, scale=-0.5).then_inc(s_rstd, 1)

            def copy_z(g, e, fill="z"):
                b, used, n = fill_no(g, (fill, e))
                wait(act, s_gated, upto(K, g, e + 1 if is_next((fill, e)) else e + 1 - K))
                wait(act, s_filled, n + 1)
                nc.scalar.activation(z[:, e], bank[:, b], ACT.Copy).then_inc(s_free[b], 1)

            def xn_tile(g, k):
                i, p = g
                b, used, n = fill_no(g, ("turn", k))
                wait(act, s_filled, n + 1)
                for j in range(SEQS):
                    col = i * (2 * SEQS) + ((p + 1) * SEQS + j)
                    a = nc.scalar.activation(xnt[:, k, j * T:(j + 1) * T], bank[:, b, j * T:(j + 1) * T],
                                             ACT.Identity, scale=xn_scale[:, k, bass.ds(col, 1)],
                                             bias=xn_shift[:, k, bass.ds(col, 1)])
                a.then_inc(s_free[b], 1)

            def first_tap(g, e):
                b, used, n = fill_no(g, ("conv", e))
                wait(act, s_filled, n + 1)
                nc.scalar.activation(u[1 - g[1]][:, e], bank[:, b], ACT.Identity, scale=conv_k[:, e, DC - 1:DC],
                                     bias=conv_c[:, e:e + 1]).then_inc(s_tap, 1)

            def silu_u(g, half):
                for e in (KH * half + KH - 2, KH * half + KH - 1):
                    b, used, n = fill_no(g, ("conv", e))
                    wait(act, s_free[b], used + 1)
                t = u[1 - g[1]][:, half * KH:half * KH + KH]
                nc.scalar.activation(t, t, ACT.Silu).then_inc(s_u, 1)

            def silu_z(g, half, first):
                if half == 0:
                    b, used, n = fill_no(g, ("z0", 3) if first else ("z", K - 1))
                    wait(act, s_free[b], used + 1)
                t = z[:, half * KH:half * KH + KH]
                nc.scalar.activation(t, t, ACT.Silu).then_inc(s_z, 1)

            def copy_xdbl(g):
                b, used, n = fill_no(g, ("xdbl", 0))
                wait(act, s_bcst, upto(16, g, 16))
                wait(act, s_filled, n + 1)
                nc.scalar.activation(xdbl[0:XR, :], bank[0:XR, b], ACT.Copy).then_inc(s_free[b], 1)

            nc.scalar.preload_act_table_set(EXP_TABLES)
            g = (-1, 1)
            act.wait_ge(s_small, 16 * N_SMALL)
            nc.scalar.activation(a_neg[:], a_neg[:], ACT.Exp).then_inc(s_cond, 1)
            nc.scalar.activation(cond_s, cond_s, ACT.Silu).then_inc(s_cond, 1)
            nc.scalar.preload_act_table_set(EXP_TABLES)
            first_root(g)
            act.wait_ge(s_ada, ADA_STEPS)
            for k in range(KD):
                xn_tile(g, k)
            for e in range(K):
                first_tap(g, e)
                if e == KH + 1:
                    silu_u(g, 0)
            copy_z(g, 0)
            silu_u(g, 1)
            nc.scalar.preload_act_table_set(EXP_TABLES)
            copy_xdbl(g)
            for k in range(KH):
                for r in range(3):
                    softplus(g, k, r)
            act.wait_ge(s_set, 6)

            def group(g, first, last):
                for h in range(PAIRS):
                    if h == SILU_U and not last:
                        silu_u(g, 0)
                        silu_u(g, 1)
                        nc.scalar.preload_act_table_set(EXP_TABLES)
                    if h == (END["z0", 3] + 3 if first else SILU_Z):
                        silu_z(g, 0, first)
                        silu_z(g, 1, first)
                        nc.scalar.preload_act_table_set(EXP_TABLES)
                    decay_tile(g, 2 * h)
                    for gd, k in due(g, h, first, last, "dt", 3):
                        softplus(gd, k, 2)
                    for gd, k in due(g, h, first, last, "dt", 2):
                        softplus(gd, k, 0)
                    for gd, e in due(g, h, first, last, "z", 2):
                        copy_z(gd, e)
                    for gd, e in due(g, h, first, last, "z0", 2):
                        copy_z(gd, e, "z0")
                    if h == AT_TURN - 6 and not last:
                        first_root(g)
                    for gd, k in due(g, h, first, last, "turn", 2):
                        xn_tile(gd, k)
                    for gd, e in due(g, h, first, last, "conv", 2):
                        first_tap(gd, e)
                    for gd, _ in due(g, h, first, last, "xdbl", 2):
                        copy_xdbl(gd)
                    decay_tile(g, 2 * h + 1)
                    for gd, k in due(g, h, first, last, "dt", 2):
                        softplus(gd, k, 1)

            run_groups(act, group)

        @block.vector
        def _(dve):
            def statistics(g, b):
                if b == 0:
                    wait(dve, s_x, upto(16, after(g), 16))
                dve.bn_stats(stats[:, b], xs[:, b]).then_inc(s_ln, 1)

            def statistics_made(g):
                wait(dve, s_ln, upto(NORM_STEPS, after(g), SEQS))

            def aggregate(g):
                for b in range(SEQS):
                    dve.bn_aggr(moments[:, b], stats[:, b]).then_inc(s_ln, 1)
                wait(dve, s_ln, upto(NORM_STEPS, after(g), 2 * SEQS))
                dve.tensor_scalar(var_eps[:], moments[:, :, 1], EPS, None, ALU.add).then_inc(s_ln, 1)

            def root(g):
                ga = after(g)
                at = 2 * SEQS + 1
                wait(dve, s_rstd, upto(2, ga, 2))
                dve.tensor_tensor(newton[:], rstd[:], rstd[:], ALU.mult).then_inc(s_ln, 1)
                wait(dve, s_ln, upto(NORM_STEPS, ga, at + 1))
                dve.tensor_tensor(newton[:], newton[:], var_eps[:], ALU.mult).then_inc(s_ln, 1)
                wait(dve, s_ln, upto(NORM_STEPS, ga, at + 2))
                dve.tensor_scalar(newton[:], newton[:], -0.5, 1.5, ALU.mult, ALU.add).then_inc(s_ln, 1)
                wait(dve, s_ln, upto(NORM_STEPS, ga, at + 3))
                dve.tensor_tensor(rstd[:], rstd[:], newton[:], ALU.mult).then_inc(s_ln, 1)

            def normalise(g, b):
                if b == 0:
                    wait(dve, s_ln, upto(NORM_STEPS, after(g), 2 * SEQS + 5))
                dve.tensor_scalar(xs[:, b], xs[:, b], moments[:, b, 0:1], rstd[:, b:b + 1],
                                  ALU.subtract, ALU.mult).then_inc(s_ln, 1)

            def tap(g, e, j):
                b, used, n = fill_no(g, ("conv", e))
                back = j + 1
                if j == 0:
                    wait(dve, s_tap, upto(K, after(g), e + 1))
                else:
                    wait(dve, s_conv, upto(2 * K, after(g), 2 * e + j))
                acc = seq3(u[1 - g[1]][:, e])[:, :, back:T]
                t = dve.scalar_tensor_tensor(acc, seq3(bank[:, b])[:, :, 0:T - back],
                                             conv_k[:, e, DC - 1 - back:DC - back], acc, ALU.mult, ALU.add)
                if back < DC - 1:
                    t.then_inc(s_conv, 1)
                else:
                    t.then_inc(s_free[b], 1)

            def finish_dt(g, k, r):
                ga = g if k >= KH else after(g)
                b, used, n = fill_no(g, ("dt", k))
                if r == 0:
                    wait(dve, s_sp, upto(3 * K, ga, 3 * k + 3))
                    if k < KH:
                        dve.tensor_tensor(dt[:, k], dt[:, k], v[:, k], ALU.add).then_inc(s_dt, 1)
                    else:
                        dve.scalar_tensor_tensor(dt[:, k], bank[:, b], 0.0, dt[:, k], ALU.max, ALU.add) \
                            .then_inc(s_free[b], 1)
                else:
                    if k < KH:
                        wait(dve, s_dt, upto(2 * K, ga, 2 * k + 1))
                    else:
                        wait(dve, s_free[b], used + 1)
                    if k == 0:
                        wait(dve, s_u, upto(2, ga, 2))
                    dve.tensor_tensor(v[:, k], dt[:, k], u[ga[1]][:, k], ALU.mult).then_inc(s_dt, 1 if k < KH else 2)

            def drive(g, h):
                if h == PAIRS:
                    g, h = after(g), 0
                s = h // 2
                half, n = s // N, s % N
                k = half * KH + 2 * (h % 2)
                if n == 0:
                    wait(dve, s_dt, upto(2 * K, g, 2 * (k + 2)))
                wait(dve, s_sum, upto(UNITS, g, 2 * h + 2 - NSLOT))
                if h % 2 == 0:
                    wait(dve, s_bc[s % NBC], upto(16 * (STEPS // NBC), g, 16 * (s // NBC + 1)))
                at = 2 * h % NSLOT
                dve.tensor_tensor(hbuf[:, at:at + 2], v[:, k:k + 2],
                                  bc[:, s % NBC, 0].unsqueeze(1).broadcast_to([P, 2, TOK]), ALU.mult) \
                    .then_inc(s_drive, 1)

            def scan(g, c):
                t = hbuf[:, c % NSLOT]
                if c % 2 == 0:
                    wait(dve, s_drive, upto(PAIRS, g, c // 2 + 1))
                wait(dve, s_decay, upto(UNITS, g, c + 1))
                dve.tensor_tensor_scan(t, decay[:, c % 2], t, 0.0, ALU.mult, ALU.add).then_inc(s_scan, 1)

            def take_y(g, half, kb):
                k = half * KH + kb
                wait(dve, s_sum, upto(UNITS, g, 4 * (half * N + N - 1) + kb + 1))
                dve.scalar_tensor_tensor(u[g[1]][:, k], u[g[1]][:, k], d_skip[:, k:k + 1], y_acc[:, kb],
                                         ALU.mult, ALU.add).then_inc(s_y, 1)

            def gate_out(g, b):
                bk, used, n = fill_no(g, ("out", b))
                if b == 0:
                    wait(dve, s_res, upto(32, before(g), 32))
                wait(dve, s_filled, n + 1)
                dve.tensor_tensor(gate_bc[:, b], bank[:, bk], gate_bc[:, b], ALU.mult).then_inc(s_free[bk], 1)

            dve.memset(w_dt[:], 0.0).then_inc(s_set, 1)
            dve.memset(xdbl[:], 0.0).then_inc(s_set, 1)
            dve.wait_ge(s_set, 2)
            dve.memset(xdbl[XR:XR + 1, :], 1.0).then_inc(s_set, 1)
            dve.memset(decay[:], 0.0).then_inc(s_set, 1)
            g = (-1, 1)
            for b in range(SEQS):
                statistics(g, b)
            statistics_made(g)
            aggregate(g)
            root(g)
            for b in range(SEQS):
                normalise(g, b)
            dve.wait_ge(s_cond, 1)
            dve.tensor_scalar(a_neg[:], a_neg[:], -1.0, None, ALU.mult).then_inc(s_set, 2)
            dve.wait_ge(s_small, 16 * N_SMALL)
            done = 0
            dve.tensor_scalar(ada_bias[:, KD:2 * KD], ada_bias[:, KD:2 * KD], 1.0, None, ALU.add).then_inc(s_ada, 1)
            done += 1
            dve.wait_ge(s_ada, done)
            for k in range(KD):
                b, used, n = fill_no(g, ("ada", k))
                dve.wait_ge(s_filled, n + 1)
                dve.tensor_scalar(xn_shift[:, k], bank[:, b, 0:NSEQ], ada_bias[:, k:k + 1], None, ALU.add).then_inc(s_ada, 1)
                done += 1
                dve.wait_ge(s_ada, done)
                dve.sem_inc(s_free[b], 1)
            for k in range(KD):
                b, used, n = fill_no(g, ("ada", KD + k))
                dve.wait_ge(s_filled, n + 1)
                dve.tensor_scalar(one_scale[:, k], bank[:, b, 0:NSEQ], ada_bias[:, KD + k:KD + k + 1], None,
                                  ALU.add).then_inc(s_ada, 1)
                done += 1
                dve.wait_ge(s_ada, done)
                dve.sem_inc(s_free[b], 1)
                dve.tensor_scalar(xn_scale[:, k], one_scale[:, k], ln_gain[:, k:k + 1], None, ALU.mult).then_inc(s_ada, 1)
                dve.scalar_tensor_tensor(xn_shift[:, k], one_scale[:, k], ln_bias[:, k:k + 1], xn_shift[:, k],
                                         ALU.mult, ALU.add).then_inc(s_ada, 1)
                done += 2
            assert done == ADA_STEPS
            for e in range(K):
                for j in range(3):
                    tap(g, e, j)
            for k in range(KH):
                finish_dt(g, k, 0)
                finish_dt(g, k, 1)
                if k == 1:
                    drive((0, 0), 0)
            def group(g, first, last):
                for h in range(PAIRS):
                    scan(g, 2 * h)
                    for gd, k in due(g, h, first, last, "dt", 4):
                        finish_dt(gd, k, 0)
                        if k < KH:
                            finish_dt(gd, k, 1)
                    for gd, e in due(g, h, first, last, "conv", 2):
                        tap(gd, e, 0)
                    for gd, e in due(g, h, first, last, "conv", 3):
                        tap(gd, e, 2)
                    if h == 1 and not first:
                        take_y(before(g), 1, 0)
                        take_y(before(g), 1, 1)
                    if h == 2 * N + 1:
                        take_y(g, 0, 0)
                        take_y(g, 0, 1)
                    if h < PAIRS - 1 or not last:
                        drive(g, h + 1)
                    if h == AT_TURN - 7 and not last:
                        statistics_made(g)
                    scan(g, 2 * h + 1)
                    for gd, k in due(g, h, first, last, "dt", 4):
                        if k >= KH:
                            finish_dt(gd, k, 1)
                    for gd, b in due(g, h, first, last, "out", 2):
                        gate_out(gd, b)
                    for gd, _ in due(g, h, first, last, "gate", 2):
                        b, used, n = fill_no(gd, ("gate", 0))
                        wait(dve, s_filled, n + 1)
                        dve.tensor_tensor(gate_rows, bank[:, b], gate_bias, ALU.add).then_inc(s_free[b], 1)
                    for gd, e in due(g, h, first, last, "conv", 2):
                        tap(gd, e, 1)
                    if not last:
                        if AT_TURN - 12 <= h < AT_TURN - 12 + SEQS:
                            statistics(g, h - (AT_TURN - 12))
                        if h == AT_TURN - 7:
                            aggregate(g)
                        if h == AT_TURN - 5:
                            root(g)
                        if AT_TURN - 4 <= h < AT_TURN:
                            normalise(g, h - (AT_TURN - 4))
                    if h == 1 and not first:
                        take_y(before(g), 1, 2)
                        take_y(before(g), 1, 3)
                    if h == 2 * N + 1:
                        take_y(g, 0, 2)
                        take_y(g, 0, 3)

            run_groups(dve, group)
            g = (GROUPS // 2, 0)
            for kb in range(KH):
                take_y(before(g), 1, kb)
            for b in range(SEQS):
                gate_out(g, b)

        @block.gpsimd
        def _(pool):
            def weigh(g, c):
                s = c // 4
                wait(pool, s_scan, upto(UNITS, g, c + 1))
                if c % 4 == 0:
                    wait(pool, s_bc[s % NBC], upto(16 * (STEPS // NBC), g, 16 * (s // NBC + 1)))
                nc.gpsimd.tensor_tensor(hbuf[:, c % NSLOT], hbuf[:, c % NSLOT], bc[:, s % NBC, 1],
                                        ALU.mult).then_inc(s_hc, 1)

            def gate_y(g, k):
                wait(pool, s_y, upto(K, g, k + 1))
                wait(pool, s_z, upto(2, g, k // KH + 1))
                nc.gpsimd.tensor_tensor(u[g[1]][:, k], u[g[1]][:, k], z[:, k], ALU.mult).then_inc(s_gated, 1)

            def add_residual(g, b):
                bk, used, n = fill_no(g, ("out", b))
                wait(pool, s_free[bk], used + 1)
                nc.gpsimd.tensor_tensor(x_res[:, b], x_res[:, b], gate_bc[:, b], ALU.add).then_inc(s_oadd, 1)

            pool.memset(ident[:], 0.0).then_inc(s_ident, 1)
            pool.wait_ge(s_ident, 1)
            pool.affine_select(out=ident[:], in_=ident[:], compare_op=ALU.not_equal, fill=1.0, base=0,
                               pattern=[[-1, P]], channel_multiplier=1).then_inc(s_ident, 1)

            def group(g, first, last):
                for h in range(PAIRS):
                    weigh(g, 2 * h)
                    if 2 <= h < 2 + KH and not first:
                        gate_y(before(g), KH + h - 2)
                    if 2 * N + 4 <= h < 2 * N + 4 + KH:
                        gate_y(g, h - 2 * N - 4)
                    weigh(g, 2 * h + 1)
                    for gd, b in due(g, h, first, last, "out", 3):
                        add_residual(gd, b)

            run_groups(pool, group)
            g = (GROUPS // 2, 0)
            for k in range(KH, K):
                gate_y(before(g), k)
            for b in range(SEQS):
                add_residual(g, b)


def kernel(**inputs):
    import numpy as _np
    import concourse.bacc as _bacc
    from concourse.bass_utils import run_bass_kernel_spmd as _run

    w = {k.replace("L0_cond_", ""): _np.asarray(a) for k, a in inputs.items()}

    def by_channel(a):
        return a.reshape(-1, P).T

    laid = {
        "x": w["x"], "cond_t": w["cond_2048"].T, "ln_g": by_channel(w["ln_g"]), "ln_b": by_channel(w["ln_b"]),
        "ada_wt": w["ada_w"].T, "ada_b": by_channel(w["ada_b"]),
        "gate_b": w["ada_b"][-w["ln_g"].size:], "in_proj_wt": w["in_proj_w"].T,
        "conv_w": w["conv_w"], "conv_b": by_channel(w["conv_b"]), "x_proj_wt": w["x_proj_w"].T,
        "dt_proj_wt": w["dt_proj_w"].T, "dt_proj_b": w["dt_proj_b"].reshape(1, -1),
        "a_log": w["A_log"], "d_param": by_channel(w["D_param"]), "out_proj_wt": w["out_proj_w"].T,
    }
    nc = _bacc.Bacc("TRN2", target_bir_lowering=False, num_devices=1)
    arrays, args = {}, []
    for name, a in laid.items():
        a = _np.ascontiguousarray(a)
        arrays[f"in_{name}"] = a
        args.append(nc.dram_tensor(f"in_{name}", a.shape, mybir.dt.from_np(a.dtype), kind="ExternalInput").ap())
    args.append(nc.dram_tensor("out_0", w["x"].shape, F32, kind="ExternalOutput").ap())
    mamba_program(nc, *args)
    r = _run(nc, [arrays], core_ids=[0])
    return r.results[0]["out_0"]
```
